# Optimizing a Trainium2 kernel written in Bass

```python
import numpy as np
import jax
import jax.numpy as jnp

def _softmax(x, axis=-1):
    return jax.nn.softmax(x, axis=axis)
def _gelu(x):
    return jax.nn.gelu(x, approximate=True)
def _silu(x):
    return jax.nn.silu(x)
def _sigmoid(x):
    return jax.nn.sigmoid(x)
def _layernorm(x, axis=-1, eps=1e-5):
    m = jnp.mean(x, axis=axis, keepdims=True)
    v = jnp.var(x, axis=axis, keepdims=True)
    return (x - m) / jnp.sqrt(v + eps)
def _scatter_add(tgt, idx, src, axis=0):
    return tgt.at[idx].add(src)
def _segment_sum(src, seg, n):
    return jax.ops.segment_sum(src, seg, n)

kernel_name = 'mk_adj_resnorm_d2_adj_256_1b742d'

def setup_inputs(seed: int = 0):
    np.random.seed(seed)
    _w = jnp.asarray
    def _rec_inputs():
        import jax
        import jax.numpy as jnp
        _gk = jax.random.key(seed)
        x = -0.0005207 + 1.001 * jax.random.normal(jax.random.fold_in(_gk, 1), (8192, 256), jnp.float32)
        _a = jax.random.bernoulli(jax.random.fold_in(_gk, 2), 0.00390625, (8192, 8192))
        _af = _a.astype(jnp.float32)
        _af = _af * jax.random.uniform(jax.random.fold_in(_gk, 3), (8192, 8192), jnp.float32, 0.05, 0.999999)
        adj = _af
        return x, adj
    x, adj = _rec_inputs()
    def _L0_gnn_setup():
        import jax, jax.numpy as jnp
        import numpy as np
        N = 8192
        D = 256
        DENSITY = 0.02
        key = jax.random.key(seed)
        k1, k2, k3, k4 = jax.random.split(key, 4)
        inputs = jax.random.normal(k1, (N, D), dtype=jnp.float32)
        vals = jax.random.uniform(k2, (N, N), dtype=jnp.float32, minval=0.1, maxval=1.0)
        mask = jax.random.uniform(k3, (N, N), dtype=jnp.float32) < DENSITY
        adj = jnp.where(mask, vals, 0.0)
        H_v = 0.1 * jax.random.normal(k4, (D, 1), dtype=jnp.float32)
        return {'inputs': inputs, 'adj': adj, 'H_v': H_v}
    _L0_gnn_all = _L0_gnn_setup()
    _L0_gnn_in = {k: v for k, v in _L0_gnn_all.items() if k in ('H_v', )}
    del _L0_gnn_all

    def _L1_gnn_setup():
        import jax, jax.numpy as jnp
        import numpy as np
        N = 8192
        D_IN = 256
        D_OUT = 256
        key = jax.random.key(seed)
        k1, k2, k3 = jax.random.split(key, 3)
        x = jax.random.normal(k1, (N, D_IN), dtype=jnp.float32)
        adj = jax.random.uniform(k2, (N, N), dtype=jnp.float32)
        W = jax.random.normal(k3, (D_OUT, D_IN), dtype=jnp.float32) * (1.0 / np.sqrt(D_IN))
        return {'x': x, 'adj': adj, 'W': W}
    _L1_gnn_all = _L1_gnn_setup()
    _L1_gnn_in = {k: v for k, v in _L1_gnn_all.items() if k in ('W', )}
    del _L1_gnn_all

    return {
        "x": x,
        "adj": adj,
        "L0_gnn_H_v": _L0_gnn_in["H_v"],
        "L1_gnn_W": _L1_gnn_in["W"],
    }

def reference(x, adj, L0_gnn_H_v, L1_gnn_W):
    import jax
    import jax.numpy as jnp
    def _L0_gnn_ref(inputs, adj, H_v):
        import jax, jax.numpy as jnp
        import numpy as np
        N = 8192
        D = 256
        DENSITY = 0.02
        scores = jnp.squeeze(inputs @ H_v, -1)
        mask = adj != 0.0
        logits = adj * scores[None, :]
        neg = jnp.asarray(jnp.finfo(logits.dtype).min, logits.dtype)
        logits = jnp.where(mask, logits, neg)
        m = jnp.max(logits, axis=1, keepdims=True)
        e = jnp.where(mask, jnp.exp(logits - m), 0.0)
        s = jnp.sum(e, axis=1, keepdims=True)
        weights = e / jnp.where(s > 0, s, 1.0)
        return weights @ inputs

    def _L1_gnn_ref(x, adj, W):
        import jax, jax.numpy as jnp
        import numpy as np
        N = 8192
        D_IN = 256
        D_OUT = 256
        A_hat = adj + jnp.eye(adj.shape[0], dtype=adj.dtype)
        d_inv_sqrt = jnp.sum(A_hat, axis=1) ** (-0.5)
        A_norm = d_inv_sqrt[:, None] * A_hat * d_inv_sqrt[None, :]
        support = x @ W.T
        out = A_norm @ support
        return jax.nn.relu(out)

    x = _layernorm(x + _L0_gnn_ref(x, adj, L0_gnn_H_v), axis=-1)
    x = _layernorm(x + _L1_gnn_ref(x, adj, L1_gnn_W), axis=-1)
    return x


_drawn_inputs = setup_inputs


def setup_inputs(seed=0):
    import zlib

    import numpy as np

    out = dict(_drawn_inputs(seed))
    spreads = {}
    factors = {}
    for name, (base, spread) in spreads.items():
        noise = np.random.default_rng([zlib.crc32(name.encode()), seed]).standard_normal(out[name].shape)
        drawn = base * np.exp(spread * noise) if base else spread * noise
        out[name] = jnp.asarray(drawn.astype(out[name].dtype))
    for name, factor in factors.items():
        out[name] = (out[name] * factor).astype(out[name].dtype)
    return out
```

```python
from contextlib import ExitStack
import math

import concourse.bass as bass
from concourse import mybir

ALU = mybir.AluOpType
ACT = mybir.ActivationFunctionType
F32 = mybir.dt.float32
F32R = mybir.dt.float32r
F16 = mybir.dt.float16
BF16 = mybir.dt.bfloat16
I32 = mybir.dt.int32
AX_X = mybir.AxisListType.X

P = 128
N = 8192
D = 256
NB = N // P
GROUP = 1024
TILES = GROUP // P
STEPS = N // GROUP
LOAD = 2048
LOADS = N // LOAD
SLOTS = 3
EPS = 1e-5
MASKED = -(2.0 ** 100)
EXP_SHIFT = 15.0 * math.log(2.0)
X_TOP = 2.0 ** 14
ROW = D + 4


def value(r, off):
    return SLOTS * r + off


def graph_network(nc, x, adj, h_v, w, out):
    scores_row = nc.dram_tensor("scores_row", (NB, P), F32).ap()
    y_rows = nc.dram_tensor("y_rows", (N, ROW), F32).ap()
    x1_rows = nc.dram_tensor("x1_rows", (N, ROW), F32).ap()

    with ExitStack() as ctx:
        ident = ctx.enter_context(nc.sbuf_tensor("ident", [P, P], F32))
        attention_layer(nc, x, adj, h_v, scores_row, y_rows, ident)
        convolution_layer(nc, adj, w, y_rows, x1_rows, out, ident)


def attention_layer(nc, x, adj, h_v, scores_row, y_rows, ident):
    with ExitStack() as ctx:
        def sb(name, shape, dt):
            return ctx.enter_context(nc.sbuf_tensor(name, shape, dt))

        def sem(name):
            return ctx.enter_context(nc.semaphore(name))

        x_parts = sb("x_parts", [P, NB, 2, D], F16)
        scores = sb("scores", [P, N], F32)
        logits = sb("logits", [P, SLOTS, N], F32)
        inv_gain = sb("inv_gain", [P, 1], F32)

        prepare_x(nc, x, h_v, scores_row, ident, x_parts, scores, logits, inv_gain)

        absent = sb("absent", [P, 2, GROUP], BF16)
        unused = sb("unused", [P, GROUP], BF16)
        wT_hi = sb("wT_hi", [P, 3, GROUP], F16)
        wT_lo = sb("wT_lo", [P, 3, GROUP], F16)
        x_res = sb("x_res", [P, SLOTS, D], F32)
        y = sb("y", [P, SLOTS, ROW], F32)
        step_max = sb("step_max", [P, SLOTS, STEPS], F32)
        step_exp_sum = sb("step_exp_sum", [P, SLOTS, STEPS], F32)
        step_adj_sum = sb("step_adj_sum", [P, SLOTS, STEPS], F32)
        row_max = sb("row_max", [P, SLOTS], F32)
        exp_bias = sb("exp_bias", [P, SLOTS], F32)
        present = sb("present", [P, SLOTS], F32)
        adj_sum = sb("adj_sum", [P, SLOTS], F32)
        exp_sum = sb("exp_sum", [P, SLOTS], F32)
        exp_inv = sb("exp_inv", [P, SLOTS], F32)
        factor = sb("factor", [P, SLOTS], F32)
        partial = sb("partial", [P, D], F32)
        carrier = sb("carrier", [P, 2], F32)
        stats = sb("stats", [P, 6], F32)
        mean_var = sb("mean_var", [P, 2], F32)

        turned = [ctx.enter_context(nc.psum_tensor(f"turned{i}", [P, GROUP], F32)) for i in range(2)]
        acc = [ctx.enter_context(nc.psum_tensor(f"acc{i}", [P, 2 * D], F32)) for i in range(SLOTS)]

        loaded = [sem(f"loaded{i}") for i in range(SLOTS * LOADS)]
        x_loaded = [sem(f"x_loaded{i}") for i in range(SLOTS)]
        marked = sem("marked")
        adj_summed = sem("adj_summed")
        scaled = sem("scaled")
        masked = sem("masked")
        max_found = sem("max_found")
        bias_ready = sem("bias_ready")
        exp_done = sem("exp_done")
        transposed = sem("transposed")
        hi_ready = sem("hi_ready")
        lo_ready = sem("lo_ready")
        multiplied = sem("multiplied")
        tail = sem("tail")
        slots_free = sem("slots_free")
        y_ready = sem("y_ready")
        y_stored = sem("y_stored")
        y_free = sem("y_free")

        TAIL_STEPS = 7

        def periods(eng, period):
            for t in (-2, -1, 0):
                period(0, t, t)
            with eng.Fori(0, 20) as r:
                for off in (1, 2, 3):
                    period(r, off, None)
            for t in (61, 62, 63, 64):
                period(0, t, t)

        def does(t, lag):
            return t is None or 0 <= t + lag < NB

        block = ctx.enter_context(nc.Block())

        @block.sync
        def _(sp):
            sp.sem_inc(y_free, SLOTS)

            def load(r, off, c):
                sp.dma_start(logits[:, off % SLOTS, c * LOAD:(c + 1) * LOAD],
                             adj[bass.ds(value(r, off) * P, P), c * LOAD:(c + 1) * LOAD]
                             ).then_inc(loaded[(off % SLOTS) * LOADS + c], 16)

            def store(r, off):
                sp.wait_ge(y_ready, value(r, off) + 1)
                sp.dma_start(y_rows[bass.ds(value(r, off) * P, P), :],
                             y[:, off % SLOTS, :]).then_inc(y_stored, 16)

            def period(r, off, t):
                if t == -2:
                    for b in range(SLOTS):
                        for c in range(LOADS):
                            load(0, b, c)
                    return
                if does(t, 0):
                    sp.wait_ge(slots_free, value(r, off) + 1)
                    sp.dma_start(x_res[:, off % SLOTS, :], x[bass.ds(value(r, off) * P, P), :]
                                 ).then_inc(x_loaded[off % SLOTS], 16)
                for c in range(LOADS):
                    if does(t, 0) and does(t, SLOTS):
                        sp.wait_ge(transposed, STEPS * value(r, off) + 2 * c + 2)
                        load(r, off + SLOTS, c)
                    if c == 2 and does(t, -1):
                        store(r, off - 1)
                if does(t, -1):
                    sp.wait_ge(y_stored, 16 * value(r, off))
                    sp.sem_inc(y_free, 1)

            periods(sp, period)

        @block.gpsimd
        def _(pool):
            def period(r, off, t):
                if not does(t, 2):
                    return
                u = (off + 2) % SLOTS
                for k in range(STEPS):
                    part = logits[:, u, k * GROUP:(k + 1) * GROUP]
                    pool.wait_ge(marked, STEPS * value(r, off + 2) + k + 1)
                    pool.wait_ge(adj_summed, STEPS * value(r, off + 2) + k + 1)
                    pool.tensor_tensor(part, part, scores[:, k * GROUP:(k + 1) * GROUP],
                                       ALU.mult).then_inc(scaled, 1)

            periods(pool, period)

        @block.scalar
        def _(act):
            def period(r, off, t):
                g = STEPS * value(r, off)
                u0, u1, u2 = (off % SLOTS, (off + 1) % SLOTS, (off + 2) % SLOTS)
                for k in range(STEPS):
                    cols = slice(k * GROUP, (k + 1) * GROUP)
                    if does(t, 2):
                        if k % 2 == 0:
                            act.wait_ge(loaded[u2 * LOADS + k // 2],
                                        16 * (r + (off + 2) // SLOTS + 1))
                        if not (t == -2 and k == 0):
                            act.wait_ge(adj_summed, g + 2 * STEPS + k)
                        act.activation(unused[:, :], logits[:, u2, cols], ACT.Identity,
                                       accum_out=step_adj_sum[:, u2, k:k + 1]).then_inc(adj_summed, 1)
                    if does(t, 0):
                        act.wait_ge(transposed, g + k + 1)
                        if t != 0 or k >= 3:
                            act.wait_ge(multiplied, g + k - 2)
                        act.activation(wT_hi[:, (off * STEPS + k) % 3, :], turned[k % 2][:, :],
                                       ACT.Copy).then_inc(hi_ready, 1)
                    if does(t, 1):
                        if k == 0:
                            act.wait_ge(bias_ready, value(r, off + 1) + 1)
                            act.wait_ge(slots_free, value(r, off + 1) + 1)
                        act.activation(logits[:, u1, cols], logits[:, u1, cols], ACT.Exp,
                                       bias=exp_bias[:, u1:u1 + 1],
                                       accum_out=step_exp_sum[:, u1, k:k + 1]).then_inc(exp_done, 1)

            periods(act, period)

        @block.vector
        def _(dve):
            dve.sem_inc(slots_free, SLOTS)

            def mark(r, off, k):
                u, g = off % SLOTS, STEPS * value(r, off) + k
                if k % 2 == 0:
                    dve.wait_ge(loaded[u * LOADS + k // 2], 16 * (r + off // SLOTS + 1))
                if not (off < SLOTS and isinstance(r, int) and g < 2):
                    dve.wait_ge(masked, g - 1)
                dve.tensor_scalar(absent[:, k % 2, :], logits[:, u, k * GROUP:(k + 1) * GROUP],
                                  0.0, MASKED, ALU.is_equal, ALU.mult).then_inc(marked, 1)

            def mask(r, off, k):
                u, g = off % SLOTS, STEPS * value(r, off) + k
                part = logits[:, u, k * GROUP:(k + 1) * GROUP]
                dve.wait_ge(marked, g + 1)
                dve.wait_ge(scaled, g + 1)
                dve.memset(carrier[:, k % 2:k % 2 + 1], 0.0)
                dve.tensor_tensor_reduce(part, part, absent[:, k % 2, :], 1.0, 2 * MASKED,
                                         ALU.add, ALU.max,
                                         step_max[:, u, k:k + 1]).then_inc(masked, 1)

            def finish_max(r, off):
                u, b = off % SLOTS, value(r, off)
                dve.wait_ge(masked, STEPS * b + STEPS)
                dve.tensor_reduce(row_max[:, u:u + 1], step_max[:, u, :], AX_X,
                                  ALU.max).then_inc(max_found, 1)
                dve.wait_ge(adj_summed, STEPS * b + STEPS)
                dve.tensor_reduce(adj_sum[:, u:u + 1], step_adj_sum[:, u, :], AX_X, ALU.add)
                dve.wait_ge(max_found, b + 1)
                dve.tensor_scalar(present[:, u:u + 1], row_max[:, u:u + 1], MASKED / 2,
                                  inv_gain[:, 0:1], ALU.is_gt, ALU.mult)
                dve.tensor_scalar(exp_bias[:, u:u + 1], row_max[:, u:u + 1], -1.0, EXP_SHIFT,
                                  ALU.mult, ALU.add).then_inc(bias_ready, 1)

            def split(r, off, k):
                g = STEPS * value(r, off) + k
                n = (off * STEPS + k) % 3
                dve.wait_ge(hi_ready, g + 1)
                dve.tensor_tensor(wT_lo[:, n, :], turned[k % 2][:, :], wT_hi[:, n, :],
                                  ALU.subtract).then_inc(lo_ready, 1)

            def finish_block(r, off):
                u, b = off % SLOTS, value(r, off)

                def follows(ins, n):
                    ins.then_inc(tail, 1)
                    dve.wait_ge(tail, TAIL_STEPS * b + n)

                dve.wait_ge(exp_done, STEPS * b + STEPS)
                dve.wait_ge(bias_ready, b + 1)
                follows(dve.tensor_reduce(exp_sum[:, u:u + 1], step_exp_sum[:, u, :], AX_X,
                                          ALU.add), 1)
                follows(dve.reciprocal(exp_inv[:, u:u + 1], exp_sum[:, u:u + 1]), 2)
                dve.wait_ge(y_free, b + 1)
                dve.tensor_scalar(y[:, u, D:D + 1], adj_sum[:, u:u + 1], 1.0, None, ALU.add)
                follows(dve.tensor_tensor(factor[:, u:u + 1], exp_inv[:, u:u + 1],
                                          present[:, u:u + 1], ALU.mult), 3)
                dve.wait_ge(multiplied, STEPS * b + STEPS)
                dve.wait_ge(x_loaded[u], 16 * (r + off // SLOTS + 1))
                follows(dve.scalar_tensor_tensor(out=partial[:, :], in0=acc[u][:, D:2 * D],
                                                 scalar=factor[:, u:u + 1], in1=x_res[:, u, :],
                                                 op0=ALU.mult, op1=ALU.add), 4)
                follows(dve.scalar_tensor_tensor(out=y[:, u, 0:D], in0=acc[u][:, 0:D],
                                                 scalar=factor[:, u:u + 1], in1=partial[:, :],
                                                 op0=ALU.mult, op1=ALU.add), 5)
                follows(dve.bn_stats(stats[:, :], y[:, u, 0:D]), 6)
                dve.memset(y[:, u, D + 3:D + 4], 0.0)
                follows(dve.bn_aggr(mean_var[:, :], stats[:, :]), 7)
                dve.tensor_scalar(y[:, u, D + 1:D + 2], mean_var[:, 1:2], EPS, None, ALU.add)
                dve.tensor_copy(y[:, u, D + 2:D + 3], mean_var[:, 0:1]).then_inc(y_ready, 1)
                dve.sem_inc(slots_free, 1)

            def period(r, off, t):
                for k in range(STEPS):
                    if does(t, 2):
                        mark(r, off + 2, k)
                        if k:
                            mask(r, off + 2, k - 1)
                    if does(t, 0):
                        split(r, off, k)
                    if k == 3 and does(t, -1):
                        finish_block(r, off - 1)
                if does(t, 2):
                    mask(r, off + 2, STEPS - 1)
                    finish_max(r, off + 2)

            periods(dve, period)

        @block.tensor
        def _(pe):
            def turn(r, off, k):
                g = STEPS * value(r, off) + k
                u = off % SLOTS
                pe.wait_ge(exp_done, g + 1)
                for i in range(TILES):
                    at = k * GROUP + i * P
                    mm = pe.transpose(turned[k % 2][:, i * P:(i + 1) * P],
                                      logits[:, u, at:at + P], ident[:, :])
                mm.then_inc(transposed, 1)

            def period(r, off, t):
                if t == -1:
                    turn(0, 0, 0)
                    turn(0, 0, 1)
                if not does(t, 0):
                    return
                pe.wait_ge(slots_free, value(r, off) + 1)
                for k in range(STEPS):
                    n = (off * STEPS + k) % 3
                    pe.wait_ge(lo_ready, STEPS * value(r, off) + k + 1)
                    if k < STEPS - 2:
                        turn(r, off, k + 2)
                    elif does(t, 1):
                        turn(r, off + 1, k + 2 - STEPS)
                    for i in range(TILES):
                        j = k * TILES + i
                        tile = slice(i * P, (i + 1) * P)
                        pe.matmul(acc[off % SLOTS][:, :], wT_hi[:, n, tile],
                                  x_parts[:, j, :, :].rearrange("p a d -> p (a d)"),
                                  start=(j == 0), stop=(j == NB - 1), skip_group_check=True)
                        mm = pe.matmul(acc[off % SLOTS][:, D:2 * D], wT_lo[:, n, tile],
                                       x_parts[:, j, 0, :], start=False, stop=(j == NB - 1),
                                       skip_group_check=True)
                    mm.then_inc(multiplied, 1)

            periods(pe, period)


def prepare_x(nc, x, h_v, scores_row, ident, x_parts, scores, staging, inv_gain):
    QUARTER = NB // 4
    with ExitStack() as ctx:
        def sb(name, shape, dt):
            return ctx.enter_context(nc.sbuf_tensor(name, shape, dt))

        def sem(name):
            return ctx.enter_context(nc.semaphore(name))

        h_row = sb("h_row", [P, D], F32)
        product = sb("product", [P, 2, D], F32)
        score_cols = sb("score_cols", [P, NB], F32)
        score_rows = sb("score_rows", [NB, P], F32)
        part_top = sb("part_top", [P, 4], F32)
        top = sb("top", [P, 1], F32)
        small = sb("small", [1, 8], F32)
        ones = sb("ones", [1, P], F32)
        gain = sb("gain", [P, 1], F32)
        x_all = staging[:, 0:2, :].rearrange("p a (t d) -> p (a t) d", d=D)

        turned = ctx.enter_context(nc.psum_tensor("score_turned", [P, 512], F32))
        top_turned = ctx.enter_context(nc.psum_tensor("top_turned", [P, 512], F32))
        spread = ctx.enter_context(nc.psum_tensor("spread", [P, 512], F32))

        x_in = [sem(f"x_in{i}") for i in range(4)]
        h_in = sem("h_in")
        ident_zero = sem("ident_zero")
        ident_ready = sem("ident_ready")
        chain = sem("prepare_chain")
        scored = sem("scored")
        topped = sem("topped")
        score_turn = sem("score_turn")
        top_turn = sem("top_turn")
        gain_pair = sem("gain_pair")
        gain_spread = sem("gain_spread")
        gain_ready = sem("gain_ready")
        rows_ready = sem("rows_ready")
        rows_out = sem("rows_out")
        scores_in = sem("scores_in")
        hi_part = sem("hi_part")

        block = ctx.enter_context(nc.Block())

        @block.sync
        def _(sp):
            sp.dma_start(h_row[:, :], h_v.rearrange("d a -> a d").to_broadcast((P, D))
                         ).then_inc(h_in, 16)
            view = x.rearrange("(t p) d -> p t d", p=P)
            for c in range(4):
                rows = slice(c * QUARTER, (c + 1) * QUARTER)
                sp.dma_start(x_all[:, rows, :], view[:, rows, :]).then_inc(x_in[c], 16)
            sp.wait_ge(rows_ready, 1)
            sp.dma_start(scores_row, score_rows[:, :]).then_inc(rows_out, 16)
            sp.wait_ge(rows_out, 16)
            flat = scores_row.rearrange("(a t) p -> a (t p)", a=1)
            sp.dma_start(scores[:, :], flat.to_broadcast((P, N))).then_inc(scores_in, 16)
            sp.wait_ge(scores_in, 16)

        @block.gpsimd
        def _(pool):
            pool.memset(ident[:, :], 0.0).then_inc(ident_zero, 1)
            pool.wait_ge(ident_zero, 1)
            pool.affine_select(out=ident[:, :], in_=ident[:, :], compare_op=ALU.not_equal, fill=1.0,
                               base=0, pattern=[[-1, P]], channel_multiplier=1).then_inc(ident_ready, 1)

        @block.vector
        def _(dve):
            links = [0]

            def follows(ins):
                links[0] += 1
                ins.then_inc(chain, 1)
                dve.wait_ge(chain, links[0])

            dve.memset(ones[:, :], 1.0)
            dve.wait_ge(h_in, 16)
            for c in range(4):
                dve.wait_ge(x_in[c], 16)
                rows = slice(c * QUARTER, (c + 1) * QUARTER)
                ins = dve.tensor_reduce(part_top[:, c:c + 1], x_all[:, rows, :],
                                        mybir.AxisListType.XY, ALU.max, apply_absolute_value=True)
            follows(ins)
            dve.tensor_reduce(top[:, :], part_top[:, :], AX_X, ALU.max).then_inc(topped, 1)
            for t in range(NB):
                if t >= 2:
                    dve.wait_ge(scored, t - 1)
                dve.tensor_tensor_reduce(product[:, t % 2, :], x_all[:, t, :], h_row[:, :], 1.0, 0.0,
                                         ALU.mult, ALU.add, score_cols[:, t:t + 1]
                                         ).then_inc(scored, 1)
            dve.wait_ge(top_turn, 1)
            follows(dve.tensor_reduce(small[:, 0:1], top_turned[0:1, 0:P], AX_X, ALU.max))
            follows(dve.tensor_scalar(small[:, 1:2], small[:, 0:1], 2.0 ** -100, None, ALU.max))
            follows(dve.tensor_scalar(small[:, 2:3].bitcast(I32), small[:, 1:2].bitcast(I32),
                                      0x7F800000, None, ALU.bitwise_and))
            follows(dve.reciprocal(small[:, 3:4], small[:, 2:3]))
            dve.tensor_scalar(small[:, 5:6], small[:, 2:3], 1.0 / X_TOP, None, ALU.mult)
            dve.tensor_scalar(small[:, 4:5], small[:, 3:4], X_TOP, None, ALU.mult
                              ).then_inc(gain_pair, 1)
            dve.wait_ge(score_turn, 1)
            dve.tensor_copy(score_rows[:, :], turned[0:NB, 0:P]).then_inc(rows_ready, 1)
            dve.wait_ge(gain_spread, 1)
            dve.tensor_copy(inv_gain[:, :], spread[:, 1:2])
            dve.tensor_copy(gain[:, :], spread[:, 0:1]).then_inc(gain_ready, 1)
            dve.wait_ge(gain_ready, 1)
            for c in range(4):
                dve.wait_ge(hi_part, c + 1)
                rows = slice(c * QUARTER, (c + 1) * QUARTER)
                dve.scalar_tensor_tensor(out=x_parts[:, rows, 1, :], in0=x_all[:, rows, :],
                                         scalar=gain[:, 0:1], in1=x_parts[:, rows, 0, :],
                                         op0=ALU.mult, op1=ALU.subtract)

        @block.scalar
        def _(act):
            act.wait_ge(gain_ready, 1)
            for c in range(4):
                rows = slice(c * QUARTER, (c + 1) * QUARTER)
                act.activation(x_parts[:, rows, 0, :], x_all[:, rows, :], ACT.Copy,
                               scale=gain[:, 0:1]).then_inc(hi_part, 1)

        @block.tensor
        def _(pe):
            pe.wait_ge(ident_ready, 1)
            pe.wait_ge(topped, 1)
            pe.transpose(top_turned[0:1, 0:P], top[:, 0:1], ident[:, :]).then_inc(top_turn, 1)
            pe.wait_ge(scored, NB)
            pe.transpose(turned[0:NB, 0:P], score_cols[:, :], ident[:, :]).then_inc(score_turn, 1)
            pe.wait_ge(gain_pair, 1)
            pe.matmul(spread[:, 0:2], ones[:, :], small[:, 4:6], start=True, stop=True
                      ).then_inc(gain_spread, 1)


def convolution_layer(nc, adj, w, y_rows, x1_rows, out, ident):
    with ExitStack() as ctx:
        support = ctx.enter_context(nc.sbuf_tensor("support", [P, NB, 2, D], F32R))
        prepare_support(nc, w, y_rows, x1_rows, ident, support)
        aggregate(nc, adj, x1_rows, out, ident, support)


def prepare_support(nc, w, y_rows, x1_rows, ident, support):
    BUFS = 4
    with ExitStack() as ctx:
        def sb(name, shape, dt):
            return ctx.enter_context(nc.sbuf_tensor(name, shape, dt))

        def sem(name):
            return ctx.enter_context(nc.semaphore(name))

        w_in = sb("w_in", [P, 2, D], F32)
        wT = sb("wT", [P, 2, D], F32)
        y = sb("y_again", [P, BUFS, ROW], F32)
        root = sb("root", [P, BUFS, 2], F32)
        x1 = sb("x1", [P, BUFS, ROW], F32)
        x1T = sb("x1T", [P, BUFS, D], F32)
        w_turned = ctx.enter_context(nc.psum_tensor("w_turned", [P, 2 * D], F32))
        turned = [ctx.enter_context(nc.psum_tensor(f"x1_turned{i}", [P, 512], F32)) for i in range(2)]
        product = [ctx.enter_context(nc.psum_tensor(f"product{i}", [P, 512], F32)) for i in range(2)]

        w_loaded = sem("w_loaded")
        w_turn = sem("w_turn")
        w_ready = sem("w_ready")
        loaded = [sem(f"y_loaded{i}") for i in range(BUFS)]
        rooted = sem("rooted")
        inverted = sem("inverted")
        x1_ready = sem("x1_ready")
        x1_stored = [sem(f"x1_stored{i}") for i in range(BUFS)]
        turn_done = sem("turn_done")
        x1T_ready = sem("x1T_ready")
        product_done = sem("product_done")
        support_hi = sem("support_hi")
        support_lo = sem("support_lo")

        def periods(eng, period):
            for t in (-2, -1, 0, 1, 2):
                period(0, t, t)
            with eng.Fori(0, 13) as r:
                for off in (3, 4, 5, 6):
                    period(r, off, None)
            for t in range(55, NB):
                period(0, t, t)

        def does(t, lag):
            return t is None or 0 <= t + lag < NB

        block = ctx.enter_context(nc.Block())

        @block.sync
        def _(sp):
            sp.dma_start(w_in[:, :, :], w.rearrange("(a p) d -> p a d", p=P)).then_inc(w_loaded, 16)

            def load(r, off):
                b = BUFS * r + off
                sp.dma_start(y[:, off % BUFS, :], y_rows[bass.ds(b * P, P), :]
                             ).then_inc(loaded[off % BUFS], 16)

            def period(r, off, t):
                if t == -2:
                    for b in range(BUFS):
                        load(0, b)
                if does(t, 2):
                    b = BUFS * r + off + 2
                    sp.wait_ge(x1_ready, b + 1)
                    sp.dma_start(x1_rows[bass.ds(b * P, P), :], x1[:, (off + 2) % BUFS, :]
                                 ).then_inc(x1_stored[(off + 2) % BUFS], 16)
                    if does(t, 2 + BUFS):
                        load(r, off + 2 + BUFS)

            periods(sp, period)
            for i in range(BUFS):
                sp.wait_ge(x1_stored[i], 16 * (NB // BUFS))

        @block.scalar
        def _(act):
            def period(r, off, t):
                b = BUFS * r + off
                if does(t, 2):
                    u = (off + 2) % BUFS
                    act.wait_ge(loaded[u], 16 * (r + (off + 2) // BUFS + 1))
                    if t is None or t + 2 >= BUFS:
                        act.wait_ge(inverted, b + 2 - BUFS + 1)
                    act.activation(root[:, u, :], y[:, u, D:D + 2], ACT.Sqrt).then_inc(rooted, 1)
                if does(t, 1):
                    act.wait_ge(turn_done, b + 2)
                    if t is None or t + 1 >= BUFS:
                        act.wait_ge(product_done, b + 1 - BUFS + 1)
                    act.activation(x1T[:, (off + 1) % BUFS, :], turned[(off + 1) % 2][:, 0:D],
                                   ACT.Copy).then_inc(x1T_ready, 1)
                if does(t, 0):
                    act.wait_ge(product_done, b + 1)
                    act.activation(support[:, bass.ds(b, 1), 0, :].rearrange("p a d -> p (a d)"),
                                   product[off % 2][:, 0:D], ACT.Copy,
                                   scale=x1[:, off % BUFS, D:D + 1]).then_inc(support_hi, 1)

            periods(act, period)

        @block.vector
        def _(dve):
            dve.wait_ge(w_turn, 1)
            dve.tensor_copy(wT[:, :, :].rearrange("p a d -> p (a d)"), w_turned[:, :]
                            ).then_inc(w_ready, 1)

            def period(r, off, t):
                b = BUFS * r + off
                if does(t, 2):
                    u = (off + 2) % BUFS
                    dve.wait_ge(rooted, b + 3)
                    if t is None or t + 2 >= BUFS:
                        dve.wait_ge(x1_stored[u], 16 * (r + (off + 2) // BUFS))
                        dve.wait_ge(turn_done, b + 2 - BUFS + 1)
                        dve.wait_ge(support_hi, b + 2 - BUFS + 1)
                    dve.reciprocal(x1[:, u, D:D + 2], root[:, u, :]).then_inc(inverted, 1)
                    dve.wait_ge(inverted, b + 3)
                    dve.tensor_copy(x1[:, u, D + 2:D + 4], y[:, u, D + 2:D + 4])
                    dve.tensor_scalar(x1[:, u, 0:D], y[:, u, 0:D], y[:, u, D + 2:D + 3],
                                      x1[:, u, D + 1:D + 2], ALU.subtract, ALU.mult
                                      ).then_inc(x1_ready, 1)
                if does(t, 0):
                    dve.wait_ge(support_hi, b + 1)
                    hi = support[:, bass.ds(b, 1), 0, :].rearrange("p a d -> p (a d)")
                    lo = support[:, bass.ds(b, 1), 1, :].rearrange("p a d -> p (a d)")
                    dve.scalar_tensor_tensor(out=lo, in0=product[off % 2][:, 0:D],
                                             scalar=x1[:, off % BUFS, D:D + 1], in1=hi.bitcast(F32),
                                             op0=ALU.mult, op1=ALU.subtract).then_inc(support_lo, 1)

            periods(dve, period)

        @block.tensor
        def _(pe):
            pe.wait_ge(w_loaded, 16)
            for k in range(2):
                for m in range(2):
                    mm = pe.transpose(w_turned[:, k * D + m * P:k * D + (m + 1) * P],
                                      w_in[:, m, k * P:(k + 1) * P], ident[:, :])
            mm.then_inc(w_turn, 1)
            pe.wait_ge(w_ready, 1)

            def period(r, off, t):
                b = BUFS * r + off
                if does(t, 1):
                    pe.wait_ge(x1_ready, b + 2)
                    if t is None or t + 1 >= 2:
                        pe.wait_ge(x1T_ready, b + 1 - 2 + 1)
                    for k in range(2):
                        mm = pe.transpose(turned[(off + 1) % 2][:, k * P:(k + 1) * P],
                                          x1[:, (off + 1) % BUFS, k * P:(k + 1) * P], ident[:, :])
                    mm.then_inc(turn_done, 1)
                if does(t, 0):
                    pe.wait_ge(x1T_ready, b + 1)
                    if t is None or t >= 2:
                        pe.wait_ge(support_lo, b - 2 + 1)
                    for k in range(2):
                        mm = pe.matmul(product[off % 2][:, 0:D],
                                       x1T[:, off % BUFS, k * P:(k + 1) * P], wT[:, k, :],
                                       start=(k == 0), stop=(k == 1))
                    mm.then_inc(product_done, 1)

            periods(pe, period)


def aggregate(nc, adj, x1_rows, out, ident, support):
    RING = 6
    with ExitStack() as ctx:
        def sb(name, shape, dt):
            return ctx.enter_context(nc.sbuf_tensor(name, shape, dt))

        def sem(name):
            return ctx.enter_context(nc.semaphore(name))

        rows = sb("rows", [P, RING, LOAD], F32)
        aT_hi = sb("aT_hi", [P, 3, GROUP], F32R)
        aT_lo = sb("aT_lo", [P, 3, GROUP], F32R)
        x1 = sb("x1_again", [P, SLOTS, ROW], F32)
        own = sb("own", [P, D], F32)
        carrier = sb("carrier1", [P, 1], F32)
        total_lo = sb("total_lo", [P, D], F32)
        total = sb("total", [P, D], F32)
        message = sb("message", [P, SLOTS, D], F32)
        y = sb("y1", [P, D], F32)
        stats = sb("stats1", [P, 6], F32)
        mean_var = sb("mean_var1", [P, 2], F32)
        eps = sb("eps", [P, 1], F32)
        root = sb("root1", [P, 1], F32)
        rstd = sb("rstd1", [P, 1], F32)
        result = sb("result", [P, SLOTS, D], F32)

        turned = [ctx.enter_context(nc.psum_tensor(f"a_turned{i}", [P, GROUP], F32)) for i in range(2)]
        acc = [ctx.enter_context(nc.psum_tensor(f"a_acc{i}", [P, 2 * D], F32)) for i in range(SLOTS)]

        loaded = [sem(f"a_loaded{i}") for i in range(RING)]
        x1_loaded = [sem(f"x1_loaded{i}") for i in range(SLOTS)]
        transposed = sem("a_transposed")
        hi_ready = sem("a_hi_ready")
        lo_ready = sem("a_lo_ready")
        multiplied = sem("a_multiplied")
        totalled = sem("totalled")
        message_ready = sem("message_ready")
        varied = sem("varied")
        rooted = sem("a_rooted")
        tail = sem("a_tail")
        slots_free = sem("a_slots_free")
        stored = sem("stored")
        result_free = sem("result_free")

        TAIL_STEPS = 6

        def periods(eng, period):
            for t in (-1, 0):
                period(0, t, t)
            with eng.Fori(0, 20) as r:
                for off in (1, 2, 3):
                    period(r, off, None)
            for t in (61, 62, 63, 64):
                period(0, t, t)

        def does(t, lag):
            return t is None or 0 <= t + lag < NB

        block = ctx.enter_context(nc.Block())

        @block.sync
        def _(sp):
            sp.sem_inc(result_free, SLOTS)

            def load(r, off, c):
                q = LOADS * off + c
                b, at = off + c // LOADS, c % LOADS * LOAD
                sp.dma_start(rows[:, q % RING, :], adj[bass.ds(value(r, b) * P, P), at:at + LOAD]
                             ).then_inc(loaded[q % RING], 16)

            def period(r, off, t):
                if t == -1:
                    for c in range(RING):
                        load(0, 0, c)
                    return
                if does(t, 0):
                    sp.wait_ge(slots_free, value(r, off) + 1)
                    sp.dma_start(x1[:, off % SLOTS, :], x1_rows[bass.ds(value(r, off) * P, P), :]
                                 ).then_inc(x1_loaded[off % SLOTS], 16)
                for c in range(LOADS):
                    if does(t, 0) and (t is None or LOADS * t + RING + c < NB * LOADS):
                        sp.wait_ge(transposed, STEPS * value(r, off) + 2 * c + 2)
                        load(r, off, RING + c)
                    if c == 2 and does(t, -1):
                        b = value(r, off - 1)
                        sp.wait_ge(tail, TAIL_STEPS * b + TAIL_STEPS)
                        sp.dma_start(out[bass.ds(b * P, P), :], result[:, (off - 1) % SLOTS, :]
                                     ).then_inc(stored, 16)
                if does(t, -1):
                    sp.wait_ge(stored, 16 * value(r, off))
                    sp.sem_inc(result_free, 1)

            periods(sp, period)

        @block.scalar
        def _(act):
            def period(r, off, t):
                for k in range(STEPS):
                    g = STEPS * value(r, off) + k
                    if does(t, 0):
                        act.wait_ge(transposed, g + 1)
                        if t != 0 or k >= 3:
                            act.wait_ge(multiplied, g - 2)
                        act.activation(aT_hi[:, (off * STEPS + k) % 3, :], turned[k % 2][:, :],
                                       ACT.Copy).then_inc(hi_ready, 1)
                    if does(t, -1) and k == 3:
                        u, b = (off - 1) % SLOTS, value(r, off - 1)
                        act.wait_ge(totalled, b + 1)
                        act.wait_ge(x1_loaded[u], 16 * (r + (off - 1) // SLOTS + 1))
                        act.activation(message[:, u, :], total[:, :], ACT.Relu,
                                       scale=x1[:, u, D:D + 1]).then_inc(message_ready, 1)
                    if does(t, -1) and k == 4:
                        act.wait_ge(varied, value(r, off - 1) + 1)
                        act.activation(root[:, :], mean_var[:, 1:2], ACT.Sqrt,
                                       bias=eps[:, 0:1]).then_inc(rooted, 1)

            periods(act, period)

        @block.vector
        def _(dve):
            dve.sem_inc(slots_free, SLOTS)
            dve.memset(eps[:, :], EPS)

            def add_parts(r, off):
                u, b = off % SLOTS, value(r, off)
                hi = support[:, bass.ds(b, 1), 0, :].rearrange("p a d -> p (a d)").bitcast(F32)
                lo = support[:, bass.ds(b, 1), 1, :].rearrange("p a d -> p (a d)").bitcast(F32)
                dve.tensor_tensor(own[:, :], hi, lo, ALU.add).then_inc(tail, 1)
                dve.wait_ge(multiplied, STEPS * b + STEPS)
                dve.wait_ge(tail, TAIL_STEPS * b + 1)
                dve.tensor_tensor(total_lo[:, :], acc[u][:, D:2 * D], own[:, :],
                                  ALU.add).then_inc(tail, 1)
                dve.wait_ge(tail, TAIL_STEPS * b + 2)
                dve.tensor_tensor(total[:, :], acc[u][:, 0:D], total_lo[:, :],
                                  ALU.add).then_inc(totalled, 1)

            def add_residual(r, off):
                u, b = off % SLOTS, value(r, off)
                dve.wait_ge(message_ready, b + 1)
                dve.tensor_tensor(y[:, :], message[:, u, :], x1[:, u, 0:D],
                                  ALU.add).then_inc(tail, 1)
                dve.wait_ge(tail, TAIL_STEPS * b + 3)
                dve.bn_stats(stats[:, :], y[:, :]).then_inc(tail, 1)
                dve.wait_ge(tail, TAIL_STEPS * b + 4)
                dve.memset(carrier[:, :], 0.0)
                dve.bn_aggr(mean_var[:, :], stats[:, :]).then_inc(varied, 1)

            def normalise(r, off):
                u, b = off % SLOTS, value(r, off)
                dve.wait_ge(rooted, b + 1)
                dve.reciprocal(rstd[:, :], root[:, :]).then_inc(tail, 1)
                dve.wait_ge(tail, TAIL_STEPS * b + 5)
                dve.wait_ge(result_free, b + 1)
                dve.tensor_scalar(result[:, u, :], y[:, :], mean_var[:, 0:1], rstd[:, 0:1],
                                  ALU.subtract, ALU.mult).then_inc(tail, 1)
                dve.sem_inc(slots_free, 1)

            def period(r, off, t):
                for k in range(STEPS):
                    if does(t, 0):
                        n = (off * STEPS + k) % 3
                        dve.wait_ge(hi_ready, STEPS * value(r, off) + k + 1)
                        dve.tensor_tensor(aT_lo[:, n, :], turned[k % 2][:, :],
                                          aT_hi[:, n, :].bitcast(F32),
                                          ALU.subtract).then_inc(lo_ready, 1)
                    if does(t, -1):
                        if k == 2:
                            add_parts(r, off - 1)
                        if k == 3:
                            add_residual(r, off - 1)
                        if k == 4:
                            normalise(r, off - 1)

            periods(dve, period)

        @block.tensor
        def _(pe):
            def turn(r, off, k):
                q = LOADS * off + k // 2
                if k % 2 == 0:
                    pe.wait_ge(loaded[q % RING], 16 * (LOADS * SLOTS // RING * r + q // RING + 1))
                for i in range(TILES):
                    at = k % 2 * GROUP + i * P
                    mm = pe.transpose(turned[k % 2][:, i * P:(i + 1) * P],
                                      rows[:, q % RING, at:at + P], ident[:, :])
                mm.then_inc(transposed, 1)

            def period(r, off, t):
                if t == -1:
                    turn(0, 0, 0)
                    turn(0, 0, 1)
                if not does(t, 0):
                    return
                pe.wait_ge(slots_free, value(r, off) + 1)
                for k in range(STEPS):
                    n = (off * STEPS + k) % 3
                    pe.wait_ge(lo_ready, STEPS * value(r, off) + k + 1)
                    if k < STEPS - 2:
                        turn(r, off, k + 2)
                    elif does(t, 1):
                        turn(r, off + 1, k + 2 - STEPS)
                    for i in range(TILES):
                        j = k * TILES + i
                        tile = slice(i * P, (i + 1) * P)
                        pe.matmul(acc[off % SLOTS][:, :], aT_hi[:, n, tile],
                                  support[:, j, :, :].rearrange("p a d -> p (a d)"),
                                  start=(j == 0), stop=(j == NB - 1), skip_group_check=True)
                        mm = pe.matmul(acc[off % SLOTS][:, D:2 * D], aT_lo[:, n, tile],
                                       support[:, j, 0, :], start=False, stop=(j == NB - 1),
                                       skip_group_check=True)
                    mm.then_inc(multiplied, 1)

            periods(pe, period)


def kernel(**inputs):
    import numpy as np
    import concourse.bacc as bacc
    from concourse.bass_utils import run_bass_kernel_spmd

    nc = bacc.Bacc("TRN2", target_bir_lowering=False, num_devices=1, dynamic_dma_scratch_size=1024)
    arrays, args = {}, []
    for name in ("x", "adj", "L0_gnn_H_v", "L1_gnn_W"):
        a = np.ascontiguousarray(inputs[name])
        arrays[f"in_{name}"] = a
        args.append(nc.dram_tensor(f"in_{name}", a.shape, mybir.dt.from_np(a.dtype),
                                   kind="ExternalInput").ap())
    out = nc.dram_tensor("out_0", (N, D), F32, kind="ExternalOutput").ap()
    graph_network(nc, *args, out)
    r = run_bass_kernel_spmd(nc, [arrays], core_ids=[0])
    return r.results[0]["out_0"]
```

```python
from contextlib import ExitStack
import math

import concourse.bass as bass
from concourse import mybir

ALU = mybir.AluOpType
ACT = mybir.ActivationFunctionType
F32 = mybir.dt.float32
F32R = mybir.dt.float32r
F16 = mybir.dt.float16
BF16 = mybir.dt.bfloat16
I32 = mybir.dt.int32
AX_X = mybir.AxisListType.X

P = 128
N = 8192
D = 256
NB = N // P
GROUP = 1024
TILES = GROUP // P
STEPS = N // GROUP
LOAD = 2048
LOADS = N // LOAD
SLOTS = 3
EPS = 1e-5
MASKED = -(2.0 ** 100)
EXP_SHIFT = 15.0 * math.log(2.0)
X_TOP = 2.0 ** 14
ROW = D + 4


def value(r, off):
    return SLOTS * r + off


def graph_network(nc, x, adj, h_v, w, out):
    scores_row = nc.dram_tensor("scores_row", (NB, P), F32).ap()
    y_rows = nc.dram_tensor("y_rows", (N, ROW), F32).ap()
    x1_rows = nc.dram_tensor("x1_rows", (N, ROW), F32).ap()

    with ExitStack() as ctx:
        ident = ctx.enter_context(nc.sbuf_tensor("ident", [P, P], F32))
        least_sum = ctx.enter_context(nc.sbuf_tensor("least_sum", [P, 1], F32))
        attention_layer(nc, x, adj, h_v, scores_row, y_rows, ident, least_sum)
        convolution_layer(nc, adj, w, y_rows, x1_rows, out, ident, least_sum)


def attention_layer(nc, x, adj, h_v, scores_row, y_rows, ident, least_sum):
    with ExitStack() as ctx:
        def sb(name, shape, dt):
            return ctx.enter_context(nc.sbuf_tensor(name, shape, dt))

        def sem(name):
            return ctx.enter_context(nc.semaphore(name))

        x_parts = sb("x_parts", [P, NB, 2, D], F16)
        scores = sb("scores", [P, N], F32)
        logits = sb("logits", [P, SLOTS, N], F32)
        inv_gain = sb("inv_gain", [P, 1], F32)

        prepare_x(nc, x, h_v, scores_row, ident, x_parts, scores, logits, inv_gain)

        absent = sb("absent", [P, 2, GROUP], BF16)
        unused = sb("unused", [P, GROUP], BF16)
        wT_hi = sb("wT_hi", [P, 3, GROUP], F16)
        wT_lo = sb("wT_lo", [P, 3, GROUP], F16)
        x_res = sb("x_res", [P, SLOTS, D], F32)
        y = sb("y", [P, SLOTS, ROW], F32)
        step_max = sb("step_max", [P, SLOTS, STEPS], F32)
        step_exp_sum = sb("step_exp_sum", [P, SLOTS, STEPS], F32)
        step_adj_sum = sb("step_adj_sum", [P, SLOTS, STEPS], F32)
        row_max = sb("row_max", [P, SLOTS], F32)
        exp_bias = sb("exp_bias", [P, SLOTS], F32)
        present = sb("present", [P, SLOTS], F32)
        adj_sum = sb("adj_sum", [P, SLOTS], F32)
        exp_sum = sb("exp_sum", [P, SLOTS], F32)
        exp_inv = sb("exp_inv", [P, SLOTS], F32)
        factor = sb("factor", [P, SLOTS], F32)
        partial = sb("partial", [P, D], F32)
        carrier = sb("carrier", [P, 2], F32)
        stats = sb("stats", [P, 6], F32)
        mean_var = sb("mean_var", [P, 2], F32)

        turned = [ctx.enter_context(nc.psum_tensor(f"turned{i}", [P, GROUP], F32)) for i in range(2)]
        acc = [ctx.enter_context(nc.psum_tensor(f"acc{i}", [P, 2 * D], F32)) for i in range(SLOTS)]

        loaded = [sem(f"loaded{i}") for i in range(SLOTS * LOADS)]
        x_loaded = [sem(f"x_loaded{i}") for i in range(SLOTS)]
        marked = sem("marked")
        adj_summed = sem("adj_summed")
        scaled = sem("scaled")
        masked = sem("masked")
        max_found = sem("max_found")
        bias_ready = sem("bias_ready")
        exp_done = sem("exp_done")
        transposed = sem("transposed")
        hi_ready = sem("hi_ready")
        lo_ready = sem("lo_ready")
        multiplied = sem("multiplied")
        tail = sem("tail")
        slots_free = sem("slots_free")
        least_started = sem("least_started")
        y_ready = sem("y_ready")
        y_stored = sem("y_stored")
        y_free = sem("y_free")

        TAIL_STEPS = 7

        def periods(eng, period):
            for t in (-2, -1, 0):
                period(0, t, t)
            with eng.Fori(0, 20) as r:
                for off in (1, 2, 3):
                    period(r, off, None)
            for t in (61, 62, 63, 64):
                period(0, t, t)

        def does(t, lag):
            return t is None or 0 <= t + lag < NB

        block = ctx.enter_context(nc.Block())

        @block.sync
        def _(sp):
            sp.sem_inc(y_free, SLOTS)

            def load(r, off, c):
                sp.dma_start(logits[:, off % SLOTS, c * LOAD:(c + 1) * LOAD],
                             adj[bass.ds(value(r, off) * P, P), c * LOAD:(c + 1) * LOAD]
                             ).then_inc(loaded[(off % SLOTS) * LOADS + c], 16)

            def store(r, off):
                sp.wait_ge(y_ready, value(r, off) + 1)
                sp.dma_start(y_rows[bass.ds(value(r, off) * P, P), :],
                             y[:, off % SLOTS, :]).then_inc(y_stored, 16)

            def period(r, off, t):
                if t == -2:
                    for b in range(SLOTS):
                        for c in range(LOADS):
                            load(0, b, c)
                    return
                if does(t, 0):
                    sp.wait_ge(slots_free, value(r, off) + 1)
                    sp.dma_start(x_res[:, off % SLOTS, :], x[bass.ds(value(r, off) * P, P), :]
                                 ).then_inc(x_loaded[off % SLOTS], 16)
                for c in range(LOADS):
                    if does(t, 0) and does(t, SLOTS):
                        sp.wait_ge(transposed, STEPS * value(r, off) + 2 * c + 2)
                        load(r, off + SLOTS, c)
                    if c == 2 and does(t, -1):
                        store(r, off - 1)
                if does(t, -1):
                    sp.wait_ge(y_stored, 16 * value(r, off))
                    sp.sem_inc(y_free, 1)

            periods(sp, period)

        @block.gpsimd
        def _(pool):
            def period(r, off, t):
                if not does(t, 2):
                    return
                u = (off + 2) % SLOTS
                for k in range(STEPS):
                    part = logits[:, u, k * GROUP:(k + 1) * GROUP]
                    pool.wait_ge(marked, STEPS * value(r, off + 2) + k + 1)
                    pool.wait_ge(adj_summed, STEPS * value(r, off + 2) + k + 1)
                    pool.tensor_tensor(part, part, scores[:, k * GROUP:(k + 1) * GROUP],
                                       ALU.mult).then_inc(scaled, 1)

            periods(pool, period)

        @block.scalar
        def _(act):
            def period(r, off, t):
                g = STEPS * value(r, off)
                u0, u1, u2 = (off % SLOTS, (off + 1) % SLOTS, (off + 2) % SLOTS)
                for k in range(STEPS):
                    cols = slice(k * GROUP, (k + 1) * GROUP)
                    if does(t, 2):
                        if k % 2 == 0:
                            act.wait_ge(loaded[u2 * LOADS + k // 2],
                                        16 * (r + (off + 2) // SLOTS + 1))
                        if not (t == -2 and k == 0):
                            act.wait_ge(adj_summed, g + 2 * STEPS + k)
                        act.activation(unused[:, :], logits[:, u2, cols], ACT.Identity,
                                       accum_out=step_adj_sum[:, u2, k:k + 1]).then_inc(adj_summed, 1)
                    if does(t, 0):
                        act.wait_ge(transposed, g + k + 1)
                        if t != 0 or k >= 3:
                            act.wait_ge(multiplied, g + k - 2)
                        act.activation(wT_hi[:, (off * STEPS + k) % 3, :], turned[k % 2][:, :],
                                       ACT.Copy).then_inc(hi_ready, 1)
                    if does(t, 1):
                        if k == 0:
                            act.wait_ge(bias_ready, value(r, off + 1) + 1)
                            act.wait_ge(slots_free, value(r, off + 1) + 1)
                        act.activation(logits[:, u1, cols], logits[:, u1, cols], ACT.Exp,
                                       bias=exp_bias[:, u1:u1 + 1],
                                       accum_out=step_exp_sum[:, u1, k:k + 1]).then_inc(exp_done, 1)

            periods(act, period)

        @block.vector
        def _(dve):
            dve.sem_inc(slots_free, SLOTS)
            dve.memset(least_sum[:, :], 3.0e38).then_inc(least_started, 1)
            dve.wait_ge(least_started, 1)

            def mark(r, off, k):
                u, g = off % SLOTS, STEPS * value(r, off) + k
                if k % 2 == 0:
                    dve.wait_ge(loaded[u * LOADS + k // 2], 16 * (r + off // SLOTS + 1))
                if not (off < SLOTS and isinstance(r, int) and g < 2):
                    dve.wait_ge(masked, g - 1)
                dve.tensor_scalar(absent[:, k % 2, :], logits[:, u, k * GROUP:(k + 1) * GROUP],
                                  0.0, MASKED, ALU.is_equal, ALU.mult).then_inc(marked, 1)

            def mask(r, off, k):
                u, g = off % SLOTS, STEPS * value(r, off) + k
                part = logits[:, u, k * GROUP:(k + 1) * GROUP]
                dve.wait_ge(marked, g + 1)
                dve.wait_ge(scaled, g + 1)
                dve.memset(carrier[:, k % 2:k % 2 + 1], 0.0)
                dve.tensor_tensor_reduce(part, part, absent[:, k % 2, :], 1.0, 2 * MASKED,
                                         ALU.add, ALU.max,
                                         step_max[:, u, k:k + 1]).then_inc(masked, 1)

            def finish_max(r, off):
                u, b = off % SLOTS, value(r, off)
                dve.wait_ge(masked, STEPS * b + STEPS)
                dve.tensor_reduce(row_max[:, u:u + 1], step_max[:, u, :], AX_X,
                                  ALU.max).then_inc(max_found, 1)
                dve.wait_ge(adj_summed, STEPS * b + STEPS)
                dve.tensor_reduce(adj_sum[:, u:u + 1], step_adj_sum[:, u, :], AX_X, ALU.add)
                dve.wait_ge(max_found, b + 1)
                dve.tensor_scalar(present[:, u:u + 1], row_max[:, u:u + 1], MASKED / 2,
                                  inv_gain[:, 0:1], ALU.is_gt, ALU.mult)
                dve.tensor_scalar(exp_bias[:, u:u + 1], row_max[:, u:u + 1], -1.0, EXP_SHIFT,
                                  ALU.mult, ALU.add).then_inc(bias_ready, 1)

            def split(r, off, k):
                g = STEPS * value(r, off) + k
                n = (off * STEPS + k) % 3
                dve.wait_ge(hi_ready, g + 1)
                dve.tensor_tensor(wT_lo[:, n, :], turned[k % 2][:, :], wT_hi[:, n, :],
                                  ALU.subtract).then_inc(lo_ready, 1)

            def finish_block(r, off):
                u, b = off % SLOTS, value(r, off)

                def follows(ins, n):
                    ins.then_inc(tail, 1)
                    dve.wait_ge(tail, TAIL_STEPS * b + n)

                dve.wait_ge(exp_done, STEPS * b + STEPS)
                dve.wait_ge(bias_ready, b + 1)
                follows(dve.tensor_reduce(exp_sum[:, u:u + 1], step_exp_sum[:, u, :], AX_X,
                                          ALU.add), 1)
                follows(dve.reciprocal(exp_inv[:, u:u + 1], exp_sum[:, u:u + 1]), 2)
                dve.wait_ge(y_free, b + 1)
                dve.tensor_scalar(y[:, u, D:D + 1], adj_sum[:, u:u + 1], 1.0, None, ALU.add)
                dve.tensor_tensor(least_sum[:, :], least_sum[:, :], adj_sum[:, u:u + 1], ALU.min)
                follows(dve.tensor_tensor(factor[:, u:u + 1], exp_inv[:, u:u + 1],
                                          present[:, u:u + 1], ALU.mult), 3)
                dve.wait_ge(multiplied, STEPS * b + STEPS)
                dve.wait_ge(x_loaded[u], 16 * (r + off // SLOTS + 1))
                follows(dve.scalar_tensor_tensor(out=partial[:, :], in0=acc[u][:, D:2 * D],
                                                 scalar=factor[:, u:u + 1], in1=x_res[:, u, :],
                                                 op0=ALU.mult, op1=ALU.add), 4)
                follows(dve.scalar_tensor_tensor(out=y[:, u, 0:D], in0=acc[u][:, 0:D],
                                                 scalar=factor[:, u:u + 1], in1=partial[:, :],
                                                 op0=ALU.mult, op1=ALU.add), 5)
                follows(dve.bn_stats(stats[:, :], y[:, u, 0:D]), 6)
                dve.memset(y[:, u, D + 3:D + 4], 0.0)
                follows(dve.bn_aggr(mean_var[:, :], stats[:, :]), 7)
                dve.tensor_scalar(y[:, u, D + 1:D + 2], mean_var[:, 1:2], EPS, None, ALU.add)
                dve.tensor_copy(y[:, u, D + 2:D + 3], mean_var[:, 0:1]).then_inc(y_ready, 1)
                dve.sem_inc(slots_free, 1)

            def period(r, off, t):
                for k in range(STEPS):
                    if does(t, 2):
                        mark(r, off + 2, k)
                        if k:
                            mask(r, off + 2, k - 1)
                    if does(t, 0):
                        split(r, off, k)
                    if k == 3 and does(t, -1):
                        finish_block(r, off - 1)
                if does(t, 2):
                    mask(r, off + 2, STEPS - 1)
                    finish_max(r, off + 2)

            periods(dve, period)

        @block.tensor
        def _(pe):
            def turn(r, off, k):
                g = STEPS * value(r, off) + k
                u = off % SLOTS
                pe.wait_ge(exp_done, g + 1)
                for i in range(TILES):
                    at = k * GROUP + i * P
                    mm = pe.transpose(turned[k % 2][:, i * P:(i + 1) * P],
                                      logits[:, u, at:at + P], ident[:, :])
                mm.then_inc(transposed, 1)

            def period(r, off, t):
                if t == -1:
                    turn(0, 0, 0)
                    turn(0, 0, 1)
                if not does(t, 0):
                    return
                pe.wait_ge(slots_free, value(r, off) + 1)
                for k in range(STEPS):
                    n = (off * STEPS + k) % 3
                    pe.wait_ge(lo_ready, STEPS * value(r, off) + k + 1)
                    if k < STEPS - 2:
                        turn(r, off, k + 2)
                    elif does(t, 1):
                        turn(r, off + 1, k + 2 - STEPS)
                    for i in range(TILES):
                        j = k * TILES + i
                        tile = slice(i * P, (i + 1) * P)
                        pe.matmul(acc[off % SLOTS][:, :], wT_hi[:, n, tile],
                                  x_parts[:, j, :, :].rearrange("p a d -> p (a d)"),
                                  start=(j == 0), stop=(j == NB - 1), skip_group_check=True)
                        mm = pe.matmul(acc[off % SLOTS][:, D:2 * D], wT_lo[:, n, tile],
                                       x_parts[:, j, 0, :], start=False, stop=(j == NB - 1),
                                       skip_group_check=True)
                    mm.then_inc(multiplied, 1)

            periods(pe, period)


def prepare_x(nc, x, h_v, scores_row, ident, x_parts, scores, staging, inv_gain):
    QUARTER = NB // 4
    with ExitStack() as ctx:
        def sb(name, shape, dt):
            return ctx.enter_context(nc.sbuf_tensor(name, shape, dt))

        def sem(name):
            return ctx.enter_context(nc.semaphore(name))

        h_row = sb("h_row", [P, D], F32)
        product = sb("product", [P, 2, D], F32)
        score_cols = sb("score_cols", [P, NB], F32)
        score_rows = sb("score_rows", [NB, P], F32)
        part_top = sb("part_top", [P, 4], F32)
        top = sb("top", [P, 1], F32)
        small = sb("small", [1, 8], F32)
        ones = sb("ones", [1, P], F32)
        gain = sb("gain", [P, 1], F32)
        x_all = staging[:, 0:2, :].rearrange("p a (t d) -> p (a t) d", d=D)

        turned = ctx.enter_context(nc.psum_tensor("score_turned", [P, 512], F32))
        top_turned = ctx.enter_context(nc.psum_tensor("top_turned", [P, 512], F32))
        spread = ctx.enter_context(nc.psum_tensor("spread", [P, 512], F32))

        x_in = [sem(f"x_in{i}") for i in range(4)]
        h_in = sem("h_in")
        ident_zero = sem("ident_zero")
        ident_ready = sem("ident_ready")
        chain = sem("prepare_chain")
        scored = sem("scored")
        topped = sem("topped")
        score_turn = sem("score_turn")
        top_turn = sem("top_turn")
        gain_pair = sem("gain_pair")
        gain_spread = sem("gain_spread")
        gain_ready = sem("gain_ready")
        rows_ready = sem("rows_ready")
        rows_out = sem("rows_out")
        scores_in = sem("scores_in")
        hi_part = sem("hi_part")

        block = ctx.enter_context(nc.Block())

        @block.sync
        def _(sp):
            sp.dma_start(h_row[:, :], h_v.rearrange("d a -> a d").to_broadcast((P, D))
                         ).then_inc(h_in, 16)
            view = x.rearrange("(t p) d -> p t d", p=P)
            for c in range(4):
                rows = slice(c * QUARTER, (c + 1) * QUARTER)
                sp.dma_start(x_all[:, rows, :], view[:, rows, :]).then_inc(x_in[c], 16)
            sp.wait_ge(rows_ready, 1)
            sp.dma_start(scores_row, score_rows[:, :]).then_inc(rows_out, 16)
            sp.wait_ge(rows_out, 16)
            flat = scores_row.rearrange("(a t) p -> a (t p)", a=1)
            sp.dma_start(scores[:, :], flat.to_broadcast((P, N))).then_inc(scores_in, 16)
            sp.wait_ge(scores_in, 16)

        @block.gpsimd
        def _(pool):
            pool.memset(ident[:, :], 0.0).then_inc(ident_zero, 1)
            pool.wait_ge(ident_zero, 1)
            pool.affine_select(out=ident[:, :], in_=ident[:, :], compare_op=ALU.not_equal, fill=1.0,
                               base=0, pattern=[[-1, P]], channel_multiplier=1).then_inc(ident_ready, 1)

        @block.vector
        def _(dve):
            links = [0]

            def follows(ins):
                links[0] += 1
                ins.then_inc(chain, 1)
                dve.wait_ge(chain, links[0])

            dve.memset(ones[:, :], 1.0)
            dve.wait_ge(h_in, 16)
            for c in range(4):
                dve.wait_ge(x_in[c], 16)
                rows = slice(c * QUARTER, (c + 1) * QUARTER)
                ins = dve.tensor_reduce(part_top[:, c:c + 1], x_all[:, rows, :],
                                        mybir.AxisListType.XY, ALU.max, apply_absolute_value=True)
            follows(ins)
            dve.tensor_reduce(top[:, :], part_top[:, :], AX_X, ALU.max).then_inc(topped, 1)
            for t in range(NB):
                if t >= 2:
                    dve.wait_ge(scored, t - 1)
                dve.tensor_tensor_reduce(product[:, t % 2, :], x_all[:, t, :], h_row[:, :], 1.0, 0.0,
                                         ALU.mult, ALU.add, score_cols[:, t:t + 1]
                                         ).then_inc(scored, 1)
            dve.wait_ge(top_turn, 1)
            follows(dve.tensor_reduce(small[:, 0:1], top_turned[0:1, 0:P], AX_X, ALU.max))
            follows(dve.tensor_scalar(small[:, 1:2], small[:, 0:1], 2.0 ** -100, None, ALU.max))
            follows(dve.tensor_scalar(small[:, 2:3].bitcast(I32), small[:, 1:2].bitcast(I32),
                                      0x7F800000, None, ALU.bitwise_and))
            follows(dve.reciprocal(small[:, 3:4], small[:, 2:3]))
            dve.tensor_scalar(small[:, 5:6], small[:, 2:3], 1.0 / X_TOP, None, ALU.mult)
            dve.tensor_scalar(small[:, 4:5], small[:, 3:4], X_TOP, None, ALU.mult
                              ).then_inc(gain_pair, 1)
            dve.wait_ge(score_turn, 1)
            dve.tensor_copy(score_rows[:, :], turned[0:NB, 0:P]).then_inc(rows_ready, 1)
            dve.wait_ge(gain_spread, 1)
            dve.tensor_copy(inv_gain[:, :], spread[:, 1:2])
            dve.tensor_copy(gain[:, :], spread[:, 0:1]).then_inc(gain_ready, 1)
            dve.wait_ge(gain_ready, 1)
            for c in range(4):
                dve.wait_ge(hi_part, c + 1)
                rows = slice(c * QUARTER, (c + 1) * QUARTER)
                dve.scalar_tensor_tensor(out=x_parts[:, rows, 1, :], in0=x_all[:, rows, :],
                                         scalar=gain[:, 0:1], in1=x_parts[:, rows, 0, :],
                                         op0=ALU.mult, op1=ALU.subtract)

        @block.scalar
        def _(act):
            act.wait_ge(gain_ready, 1)
            for c in range(4):
                rows = slice(c * QUARTER, (c + 1) * QUARTER)
                act.activation(x_parts[:, rows, 0, :], x_all[:, rows, :], ACT.Copy,
                               scale=gain[:, 0:1]).then_inc(hi_part, 1)

        @block.tensor
        def _(pe):
            pe.wait_ge(ident_ready, 1)
            pe.wait_ge(topped, 1)
            pe.transpose(top_turned[0:1, 0:P], top[:, 0:1], ident[:, :]).then_inc(top_turn, 1)
            pe.wait_ge(scored, NB)
            pe.transpose(turned[0:NB, 0:P], score_cols[:, :], ident[:, :]).then_inc(score_turn, 1)
            pe.wait_ge(gain_pair, 1)
            pe.matmul(spread[:, 0:2], ones[:, :], small[:, 4:6], start=True, stop=True
                      ).then_inc(gain_spread, 1)


def convolution_layer(nc, adj, w, y_rows, x1_rows, out, ident, least_sum):
    with ExitStack() as ctx:
        support = ctx.enter_context(nc.sbuf_tensor("support", [P, NB, 2, D], F16))
        prepare_support(nc, w, y_rows, x1_rows, ident, least_sum, support)
        aggregate(nc, adj, x1_rows, out, ident, support)


def prepare_support(nc, w, y_rows, x1_rows, ident, least_sum, support):
    BUFS = 4
    with ExitStack() as ctx:
        def sb(name, shape, dt):
            return ctx.enter_context(nc.sbuf_tensor(name, shape, dt))

        def sem(name):
            return ctx.enter_context(nc.semaphore(name))

        w_in = sb("w_in", [P, 2, D], F32)
        w_square = sb("w_square", [P, 2, D], F32)
        w_norms = sb("w_norms", [P, 2], F32)
        extremes = sb("extremes", [P, 2], F32)
        small = sb("small1", [1, 8], F32)
        ones = sb("ones1", [1, P], F32)
        gains = sb("gains", [P, 2], F32)
        wT = sb("wT", [P, 2, D], F32)
        y = sb("y_again", [P, BUFS, ROW], F32)
        root = sb("root", [P, BUFS, 2], F32)
        dinv = sb("dinv", [P, BUFS, 2], F32)
        x1 = sb("x1", [P, BUFS, ROW], F32)
        x1T = sb("x1T", [P, BUFS, D], F32)
        w_turned = ctx.enter_context(nc.psum_tensor("w_turned", [P, 2 * D], F32))
        extremes_turned = ctx.enter_context(nc.psum_tensor("extremes_turned", [P, 512], F32))
        spread = ctx.enter_context(nc.psum_tensor("spread1", [P, 512], F32))
        turned = [ctx.enter_context(nc.psum_tensor(f"x1_turned{i}", [P, 512], F32)) for i in range(2)]
        product = [ctx.enter_context(nc.psum_tensor(f"product{i}", [P, 512], F32)) for i in range(2)]

        w_loaded = sem("w_loaded")
        w_turn = sem("w_turn")
        w_ready = sem("w_ready")
        chain = sem("gain_chain")
        extremes_ready = sem("extremes_ready")
        extremes_turn = sem("extremes_turn")
        bound_squared = sem("bound_squared")
        bound_ready = sem("bound_ready")
        gain_pair = sem("gain_pair1")
        gain_spread = sem("gain_spread1")
        gains_ready = sem("gains_ready")
        loaded = [sem(f"y_loaded{i}") for i in range(BUFS)]
        rooted = sem("rooted")
        inverted = sem("inverted")
        x1_ready = sem("x1_ready")
        x1_stored = [sem(f"x1_stored{i}") for i in range(BUFS)]
        turn_done = sem("turn_done")
        x1T_ready = sem("x1T_ready")
        product_done = sem("product_done")
        support_hi = sem("support_hi")
        support_lo = sem("support_lo")

        def periods(eng, period):
            for t in (-2, -1, 0, 1, 2):
                period(0, t, t)
            with eng.Fori(0, 13) as r:
                for off in (3, 4, 5, 6):
                    period(r, off, None)
            for t in range(55, NB):
                period(0, t, t)

        def does(t, lag):
            return t is None or 0 <= t + lag < NB

        block = ctx.enter_context(nc.Block())

        @block.sync
        def _(sp):
            sp.dma_start(w_in[:, :, :], w.rearrange("(a p) d -> p a d", p=P)).then_inc(w_loaded, 16)

            def load(r, off):
                b = BUFS * r + off
                sp.dma_start(y[:, off % BUFS, :], y_rows[bass.ds(b * P, P), :]
                             ).then_inc(loaded[off % BUFS], 16)

            def period(r, off, t):
                if t == -2:
                    for b in range(BUFS):
                        load(0, b)
                if does(t, 2):
                    b = BUFS * r + off + 2
                    sp.wait_ge(x1_ready, b + 1)
                    if does(t, 2 + BUFS):
                        load(r, off + 2 + BUFS)
                    sp.dma_start(x1_rows[bass.ds(b * P, P), :], x1[:, (off + 2) % BUFS, :]
                                 ).then_inc(x1_stored[(off + 2) % BUFS], 16)

            periods(sp, period)
            for i in range(BUFS):
                sp.wait_ge(x1_stored[i], 16 * (NB // BUFS))

        @block.scalar
        def _(act):
            act.wait_ge(bound_squared, 1)
            act.activation(small[:, 3:4], small[:, 2:3], ACT.Sqrt).then_inc(bound_ready, 1)

            def period(r, off, t):
                b = BUFS * r + off
                if does(t, 2):
                    u = (off + 2) % BUFS
                    act.wait_ge(loaded[u], 16 * (r + (off + 2) // BUFS + 1))
                    if t is None or t + 2 >= BUFS:
                        act.wait_ge(inverted, b + 2 - BUFS + 1)
                    act.activation(root[:, u, :], y[:, u, D:D + 2], ACT.Sqrt).then_inc(rooted, 1)
                if does(t, 1):
                    act.wait_ge(turn_done, b + 2)
                    if t is None or t + 1 >= BUFS:
                        act.wait_ge(product_done, b + 1 - BUFS + 1)
                    act.activation(x1T[:, (off + 1) % BUFS, :], turned[(off + 1) % 2][:, 0:D],
                                   ACT.Copy).then_inc(x1T_ready, 1)
                if does(t, 0):
                    act.wait_ge(product_done, b + 1)
                    act.activation(support[:, bass.ds(b, 1), 0, :].rearrange("p a d -> p (a d)"),
                                   product[off % 2][:, 0:D], ACT.Copy,
                                   scale=x1[:, off % BUFS, D:D + 1]).then_inc(support_hi, 1)

            periods(act, period)

        @block.vector
        def _(dve):
            links = [0]

            def follows(ins):
                links[0] += 1
                ins.then_inc(chain, 1)
                dve.wait_ge(chain, links[0])

            dve.memset(ones[:, :], 1.0)
            dve.tensor_scalar(extremes[:, 1:2], least_sum[:, :], 1.0, None, ALU.add).then_inc(chain, 1)
            links[0] += 1
            dve.wait_ge(w_loaded, 16)
            for m in range(2):
                ins = dve.tensor_tensor_reduce(w_square[:, m, :], w_in[:, m, :], w_in[:, m, :],
                                               1.0, 0.0, ALU.mult, ALU.add, w_norms[:, m:m + 1])
            follows(ins)
            follows(dve.reciprocal(extremes[:, 1:2], extremes[:, 1:2]))
            dve.tensor_reduce(extremes[:, 0:1], w_norms[:, :], AX_X, ALU.max
                              ).then_inc(extremes_ready, 1)
            dve.wait_ge(w_turn, 1)
            dve.tensor_copy(wT[:, :, :].rearrange("p a d -> p (a d)"), w_turned[:, :]
                            ).then_inc(w_ready, 1)
            dve.wait_ge(extremes_turn, 1)
            follows(dve.tensor_reduce(small[:, 0:2], extremes_turned[0:1, 0:2 * P].rearrange(
                "a (b p) -> a b p", b=2), AX_X, ALU.max))
            follows(dve.tensor_tensor(small[:, 2:3], small[:, 0:1], small[:, 1:2], ALU.mult))
            follows(dve.tensor_scalar(small[:, 2:3], small[:, 2:3], float(D), 2.0 ** -100,
                                      ALU.mult, ALU.max))
            dve.sem_inc(bound_squared, 1)
            dve.wait_ge(bound_ready, 1)
            follows(dve.tensor_scalar(small[:, 4:5].bitcast(I32), small[:, 3:4].bitcast(I32),
                                      0x7F800000, None, ALU.bitwise_and))
            follows(dve.reciprocal(small[:, 5:6], small[:, 4:5]))
            dve.tensor_scalar(small[:, 7:8], small[:, 4:5], 1.0 / X_TOP, None, ALU.mult)
            dve.tensor_scalar(small[:, 6:7], small[:, 5:6], X_TOP, None, ALU.mult
                              ).then_inc(gain_pair, 1)
            dve.wait_ge(gain_spread, 1)
            dve.tensor_copy(gains[:, :], spread[:, 0:2]).then_inc(gains_ready, 1)
            dve.wait_ge(gains_ready, 1)

            def period(r, off, t):
                b = BUFS * r + off
                if does(t, 2):
                    u = (off + 2) % BUFS
                    dve.wait_ge(rooted, b + 3)
                    if t is None or t + 2 >= BUFS:
                        dve.wait_ge(x1_stored[u], 16 * (r + (off + 2) // BUFS))
                        dve.wait_ge(turn_done, b + 2 - BUFS + 1)
                        dve.wait_ge(support_hi, b + 2 - BUFS + 1)
                    dve.reciprocal(dinv[:, u, :], root[:, u, :]).then_inc(inverted, 1)
                    dve.wait_ge(inverted, b + 3)
                    dve.tensor_scalar(x1[:, u, D:D + 2], gains[:, :], dinv[:, u, 0:1], None,
                                      ALU.mult)
                    dve.tensor_copy(x1[:, u, D + 2:D + 4], y[:, u, D + 2:D + 4])
                    dve.tensor_scalar(x1[:, u, 0:D], y[:, u, 0:D], y[:, u, D + 2:D + 3],
                                      dinv[:, u, 1:2], ALU.subtract, ALU.mult
                                      ).then_inc(x1_ready, 1)
                if does(t, 0):
                    dve.wait_ge(support_hi, b + 1)
                    hi = support[:, bass.ds(b, 1), 0, :].rearrange("p a d -> p (a d)")
                    lo = support[:, bass.ds(b, 1), 1, :].rearrange("p a d -> p (a d)")
                    dve.scalar_tensor_tensor(out=lo, in0=product[off % 2][:, 0:D],
                                             scalar=x1[:, off % BUFS, D:D + 1], in1=hi,
                                             op0=ALU.mult, op1=ALU.subtract).then_inc(support_lo, 1)

            periods(dve, period)

        @block.tensor
        def _(pe):
            pe.wait_ge(w_loaded, 16)
            for k in range(2):
                for m in range(2):
                    mm = pe.transpose(w_turned[:, k * D + m * P:k * D + (m + 1) * P],
                                      w_in[:, m, k * P:(k + 1) * P], ident[:, :])
            mm.then_inc(w_turn, 1)
            pe.wait_ge(extremes_ready, 1)
            for i in range(2):
                mm = pe.transpose(extremes_turned[0:1, i * P:(i + 1) * P], extremes[:, i:i + 1],
                                  ident[:, :])
            mm.then_inc(extremes_turn, 1)
            pe.wait_ge(gain_pair, 1)
            pe.matmul(spread[:, 0:2], ones[:, :], small[:, 6:8], start=True, stop=True
                      ).then_inc(gain_spread, 1)
            pe.wait_ge(w_ready, 1)

            def period(r, off, t):
                b = BUFS * r + off
                if does(t, 1):
                    pe.wait_ge(x1_ready, b + 2)
                    if t is None or t + 1 >= 2:
                        pe.wait_ge(x1T_ready, b + 1 - 2 + 1)
                    for k in range(2):
                        mm = pe.transpose(turned[(off + 1) % 2][:, k * P:(k + 1) * P],
                                          x1[:, (off + 1) % BUFS, k * P:(k + 1) * P], ident[:, :])
                    mm.then_inc(turn_done, 1)
                if does(t, 0):
                    pe.wait_ge(x1T_ready, b + 1)
                    if t is None or t >= 2:
                        pe.wait_ge(support_lo, b - 2 + 1)
                    for k in range(2):
                        mm = pe.matmul(product[off % 2][:, 0:D],
                                       x1T[:, off % BUFS, k * P:(k + 1) * P], wT[:, k, :],
                                       start=(k == 0), stop=(k == 1))
                    mm.then_inc(product_done, 1)

            periods(pe, period)


def aggregate(nc, adj, x1_rows, out, ident, support):
    BY_PE = {2: 0, 4: 1, 7: 0}
    PE_ORDER = sorted(BY_PE)
    BY_DMA = [k for k in range(STEPS) if k not in BY_PE]
    RING = 4
    PARTS_AHEAD, DMA_AHEAD, PE_AHEAD = 4, 3, 2

    with ExitStack() as ctx:
        def sb(name, shape, dt):
            return ctx.enter_context(nc.sbuf_tensor(name, shape, dt))

        def sem(name):
            return ctx.enter_context(nc.semaphore(name))

        rows = sb("rows", [P, SLOTS, N], F32)
        parts = sb("parts", [P, RING, 2, GROUP], F16)
        aT = sb("aT", [P, RING, 2, GROUP], F16)
        ident16 = sb("ident16", [P, P], F16)
        step_top = sb("step_top", [P, SLOTS, STEPS], F32)
        top = sb("row_top", [P, SLOTS, 3], F32)
        scale = sb("scale", [P, SLOTS], F32)
        inv_scale = sb("inv_scale", [P, SLOTS], F32)
        x1 = sb("x1_again", [P, SLOTS, ROW], F32)
        own = sb("own", [P, D], F32)
        carrier = sb("carrier1", [P, 1], F32)
        total_lo = sb("total_lo", [P, D], F32)
        total = sb("total", [P, D], F32)
        message = sb("message", [P, SLOTS, D], F32)
        y = sb("y1", [P, D], F32)
        stats = sb("stats1", [P, 6], F32)
        mean_var = sb("mean_var1", [P, 2], F32)
        eps = sb("eps", [P, 1], F32)
        root = sb("root1", [P, 1], F32)
        rstd = sb("rstd1", [P, 1], F32)
        result = sb("result", [P, SLOTS, D], F32)

        turned = [ctx.enter_context(nc.psum_tensor(f"a_turned{i}", [P, 2 * GROUP], F16)) for i in range(2)]
        acc = [ctx.enter_context(nc.psum_tensor(f"a_acc{i}", [P, 2 * D], F32)) for i in range(SLOTS)]

        loaded = [sem(f"a_loaded{i}") for i in range(SLOTS * LOADS)]
        x1_loaded = [sem(f"x1_loaded{i}") for i in range(SLOTS)]
        ident16_ready = sem("ident16_ready")
        topped = sem("a_topped")
        scaling = sem("scaling")
        scale_ready = sem("scale_ready")
        hi_ready = sem("a_hi_ready")
        lo_ready = sem("a_lo_ready")
        dma_turned = [sem(f"dma_turned{i}") for i in range(RING)]
        pe_turned = sem("pe_turned")
        evacuated = sem("evacuated")
        multiplied = sem("a_multiplied")
        totalled = sem("totalled")
        message_ready = sem("message_ready")
        varied = sem("varied")
        rooted = sem("a_rooted")
        tail = sem("a_tail")
        slots_free = sem("a_slots_free")
        carried = sem("carried")
        stored = sem("stored")
        result_free = sem("result_free")

        TAIL_STEPS = 6
        SCALING_STEPS = 4

        def periods(eng, period):
            for t in (-2, -1, 0):
                period(0, t, t)
            with eng.Fori(0, 20) as r:
                for off in (1, 2, 3):
                    period(r, off, None)
            for t in (61, 62, 63, 64):
                period(0, t, t)

        def does(t, lag):
            return t is None or 0 <= t + lag < NB

        def ahead(off, t, k, steps):
            more, k = divmod(k + steps, STEPS)
            return off + more, does(t, more), k

        def transposed_by(eng, r, off, k):
            if k in BY_PE:
                eng.wait_ge(pe_turned, len(BY_PE) * value(r, off) + PE_ORDER.index(k) + 1)
            else:
                same = [j for j in BY_DMA if j % RING == k % RING]
                eng.wait_ge(dma_turned[k % RING],
                            16 * (len(same) * value(r, off) + same.index(k) + 1))

        block = ctx.enter_context(nc.Block())

        @block.sync
        def _(sp):
            sp.sem_inc(result_free, SLOTS)

            def load(r, off, c):
                sp.dma_start(rows[:, off % SLOTS, c * LOAD:(c + 1) * LOAD],
                             adj[bass.ds(value(r, off) * P, P), c * LOAD:(c + 1) * LOAD]
                             ).then_inc(loaded[(off % SLOTS) * LOADS + c], 16)

            def turn(r, off, k):
                g = STEPS * value(r, off) + k
                sp.wait_ge(lo_ready, g + 1)
                sp.sem_inc(carried, 1)
                if not (isinstance(r, int) and g < RING):
                    sp.wait_ge(multiplied, g - RING + 1)
                    sp.sem_inc(carried, 1)
                sp.dma_start_transpose(
                    aT[:, k % RING, :, :].rearrange("p a (t i) -> p (a t) i", i=P),
                    parts[:, k % RING, :, :].rearrange("p a j -> p (a j)")
                ).then_inc(dma_turned[k % RING], 16)

            def period(r, off, t):
                if t == -2:
                    for b in range(SLOTS):
                        for c in range(LOADS):
                            load(0, b, c)
                    return
                if does(t, 0):
                    sp.wait_ge(slots_free, value(r, off) + 1)
                    sp.dma_start(x1[:, off % SLOTS, :], x1_rows[bass.ds(value(r, off) * P, P), :]
                                 ).then_inc(x1_loaded[off % SLOTS], 16)
                for k in range(STEPS):
                    o, there, kk = ahead(off, t, k, DMA_AHEAD)
                    if there and kk in BY_DMA:
                        turn(r, o, kk)
                    if k % 2 == 1 and does(t, 0) and does(t, SLOTS):
                        sp.wait_ge(lo_ready, STEPS * value(r, off) + k + 1)
                        load(r, off + SLOTS, k // 2)
                    if k == 5 and does(t, -1):
                        b = value(r, off - 1)
                        sp.wait_ge(tail, TAIL_STEPS * b + TAIL_STEPS)
                        sp.dma_start(out[bass.ds(b * P, P), :], result[:, (off - 1) % SLOTS, :]
                                     ).then_inc(stored, 16)
                if does(t, -1):
                    sp.wait_ge(stored, 16 * value(r, off))
                    sp.sem_inc(result_free, 1)

            periods(sp, period)

        @block.scalar
        def _(act):
            def high_part(r, off, k):
                g = STEPS * value(r, off) + k
                u = off % SLOTS
                act.wait_ge(scale_ready, value(r, off) + 1)
                if not (isinstance(r, int) and g < RING):
                    transposed_by(act, r, off + (k - RING) // STEPS, (k - RING) % STEPS)
                act.activation(parts[:, k % RING, 0, :], rows[:, u, k * GROUP:(k + 1) * GROUP],
                               ACT.Copy, scale=scale[:, u:u + 1]).then_inc(hi_ready, 1)

            def evacuate(r, off, k):
                m = len(BY_PE) * value(r, off) + PE_ORDER.index(k)
                g = STEPS * value(r, off) + k
                act.wait_ge(pe_turned, m + 1)
                if not (isinstance(r, int) and g < RING):
                    act.wait_ge(multiplied, g - RING + 1)
                act.activation(aT[:, k % RING, :, :].rearrange("p a j -> p (a j)"),
                               turned[BY_PE[k]][:, :], ACT.Copy).then_inc(evacuated, 1)

            def period(r, off, t):
                for k in range(STEPS):
                    o, there, kk = ahead(off, t, k, PARTS_AHEAD)
                    if there:
                        high_part(r, o, kk)
                    o, there, kk = ahead(off, t, k, PE_AHEAD)
                    if there and kk in BY_PE:
                        evacuate(r, o, kk)
                    if does(t, -1) and k == 3:
                        u, b = (off - 1) % SLOTS, value(r, off - 1)
                        act.wait_ge(totalled, b + 1)
                        act.wait_ge(x1_loaded[u], 16 * (r + (off - 1) // SLOTS + 1))
                        act.activation(message[:, u, :], total[:, :], ACT.Relu,
                                       scale=x1[:, u, D + 1:D + 2]).then_inc(message_ready, 1)
                    if does(t, -1) and k == 4:
                        act.wait_ge(varied, value(r, off - 1) + 1)
                        act.activation(root[:, :], mean_var[:, 1:2], ACT.Sqrt,
                                       bias=eps[:, 0:1]).then_inc(rooted, 1)

            periods(act, period)

        @block.vector
        def _(dve):
            dve.sem_inc(slots_free, SLOTS)
            dve.tensor_copy(ident16[:, :], ident[:, :]).then_inc(ident16_ready, 1)
            dve.memset(eps[:, :], EPS)

            def find_top(r, off, k):
                u = off % SLOTS
                if k % 2 == 0:
                    dve.wait_ge(loaded[u * LOADS + k // 2], 16 * (r + off // SLOTS + 1))
                dve.tensor_reduce(step_top[:, u, k:k + 1], rows[:, u, k * GROUP:(k + 1) * GROUP],
                                  AX_X, ALU.max, apply_absolute_value=True).then_inc(topped, 1)

            def find_scale(r, off):
                u, b = off % SLOTS, value(r, off)

                def follows(ins, n):
                    ins.then_inc(scaling, 1)
                    dve.wait_ge(scaling, SCALING_STEPS * b + n)

                dve.wait_ge(topped, STEPS * b + STEPS)
                follows(dve.tensor_reduce(top[:, u, 0:1], step_top[:, u, :], AX_X, ALU.max), 1)
                follows(dve.tensor_scalar(top[:, u, 0:1], top[:, u, 0:1], 2.0 ** -100, None,
                                          ALU.max), 2)
                follows(dve.tensor_scalar(top[:, u, 1:2].bitcast(I32), top[:, u, 0:1].bitcast(I32),
                                          0x7F800000, None, ALU.bitwise_and), 3)
                follows(dve.reciprocal(top[:, u, 2:3], top[:, u, 1:2]), 4)
                dve.tensor_scalar(inv_scale[:, u:u + 1], top[:, u, 1:2], 1.0 / X_TOP, None, ALU.mult)
                dve.tensor_scalar(scale[:, u:u + 1], top[:, u, 2:3], X_TOP, None,
                                  ALU.mult).then_inc(scale_ready, 1)

            def low_part(r, off, k):
                g = STEPS * value(r, off) + k
                u = off % SLOTS
                dve.wait_ge(hi_ready, g + 1)
                dve.scalar_tensor_tensor(out=parts[:, k % RING, 1, :],
                                         in0=rows[:, u, k * GROUP:(k + 1) * GROUP],
                                         scalar=scale[:, u:u + 1], in1=parts[:, k % RING, 0, :],
                                         op0=ALU.mult, op1=ALU.subtract).then_inc(lo_ready, 1)

            def add_parts(r, off):
                u, b = off % SLOTS, value(r, off)
                hi = support[:, bass.ds(b, 1), 0, :].rearrange("p a d -> p (a d)")
                lo = support[:, bass.ds(b, 1), 1, :].rearrange("p a d -> p (a d)")
                dve.tensor_tensor(own[:, :], hi, lo, ALU.add).then_inc(tail, 1)
                dve.wait_ge(multiplied, STEPS * b + STEPS)
                dve.wait_ge(tail, TAIL_STEPS * b + 1)
                dve.scalar_tensor_tensor(out=total_lo[:, :], in0=acc[u][:, D:2 * D],
                                         scalar=inv_scale[:, u:u + 1], in1=own[:, :],
                                         op0=ALU.mult, op1=ALU.add).then_inc(tail, 1)
                dve.wait_ge(tail, TAIL_STEPS * b + 2)
                dve.scalar_tensor_tensor(out=total[:, :], in0=acc[u][:, 0:D],
                                         scalar=inv_scale[:, u:u + 1], in1=total_lo[:, :],
                                         op0=ALU.mult, op1=ALU.add).then_inc(totalled, 1)

            def add_residual(r, off):
                u, b = off % SLOTS, value(r, off)
                dve.wait_ge(message_ready, b + 1)
                dve.tensor_tensor(y[:, :], message[:, u, :], x1[:, u, 0:D],
                                  ALU.add).then_inc(tail, 1)
                dve.wait_ge(tail, TAIL_STEPS * b + 3)
                dve.bn_stats(stats[:, :], y[:, :]).then_inc(tail, 1)
                dve.wait_ge(tail, TAIL_STEPS * b + 4)
                dve.memset(carrier[:, :], 0.0)
                dve.bn_aggr(mean_var[:, :], stats[:, :]).then_inc(varied, 1)

            def normalise(r, off):
                u, b = off % SLOTS, value(r, off)
                dve.wait_ge(rooted, b + 1)
                dve.reciprocal(rstd[:, :], root[:, :]).then_inc(tail, 1)
                dve.wait_ge(tail, TAIL_STEPS * b + 5)
                dve.wait_ge(result_free, b + 1)
                dve.tensor_scalar(result[:, u, :], y[:, :], mean_var[:, 0:1], rstd[:, 0:1],
                                  ALU.subtract, ALU.mult).then_inc(tail, 1)
                dve.sem_inc(slots_free, 1)

            def period(r, off, t):
                for k in range(STEPS):
                    o, there, kk = ahead(off, t, k, PARTS_AHEAD)
                    if there:
                        low_part(r, o, kk)
                    if does(t, 2):
                        find_top(r, off + 2, k)
                    if does(t, -1):
                        if k == 2:
                            add_parts(r, off - 1)
                        if k == 3:
                            add_residual(r, off - 1)
                        if k == 4:
                            normalise(r, off - 1)
                if does(t, 2):
                    find_scale(r, off + 2)

            periods(dve, period)

        @block.tensor
        def _(pe):
            pe.wait_ge(ident16_ready, 1)

            def turn(r, off, k):
                m = len(BY_PE) * value(r, off) + PE_ORDER.index(k)
                since = next(n for n in range(1, len(BY_PE) + 1)
                             if BY_PE[PE_ORDER[(PE_ORDER.index(k) - n) % len(BY_PE)]] == BY_PE[k])
                pe.wait_ge(lo_ready, STEPS * value(r, off) + k + 1)
                if not (isinstance(r, int) and m < since):
                    pe.wait_ge(evacuated, m - since + 1)
                for i in range(2 * TILES):
                    a, at = i // TILES, i % TILES * P
                    mm = pe.transpose(turned[BY_PE[k]][:, i * P:(i + 1) * P],
                                      parts[:, k % RING, a, at:at + P], ident16[:, :])
                mm.then_inc(pe_turned, 1)

            def turned_by(r, off, k):
                if k in BY_PE:
                    pe.wait_ge(evacuated, len(BY_PE) * value(r, off) + PE_ORDER.index(k) + 1)
                else:
                    transposed_by(pe, r, off, k)

            def period(r, off, t):
                if does(t, 0):
                    pe.wait_ge(slots_free, value(r, off) + 1)
                for k in range(STEPS):
                    o, there, kk = ahead(off, t, k, PE_AHEAD)
                    if there and kk in BY_PE:
                        turn(r, o, kk)
                    if not does(t, 0):
                        continue
                    turned_by(r, off, k)
                    for i in range(TILES):
                        j = k * TILES + i
                        tile = slice(i * P, (i + 1) * P)
                        pe.matmul(acc[off % SLOTS][:, :], aT[:, k % RING, 0, tile],
                                  support[:, j, :, :].rearrange("p a d -> p (a d)"),
                                  start=(j == 0), stop=(j == NB - 1), skip_group_check=True)
                        mm = pe.matmul(acc[off % SLOTS][:, D:2 * D], aT[:, k % RING, 1, tile],
                                       support[:, j, 0, :], start=False, stop=(j == NB - 1),
                                       skip_group_check=True)
                    mm.then_inc(multiplied, 1)

            periods(pe, period)


def kernel(**inputs):
    import numpy as np
    import concourse.bacc as bacc
    from concourse.bass_utils import run_bass_kernel_spmd

    nc = bacc.Bacc("TRN2", target_bir_lowering=False, num_devices=1, dynamic_dma_scratch_size=1024)
    arrays, args = {}, []
    for name in ("x", "adj", "L0_gnn_H_v", "L1_gnn_W"):
        a = np.ascontiguousarray(inputs[name])
        arrays[f"in_{name}"] = a
        args.append(nc.dram_tensor(f"in_{name}", a.shape, mybir.dt.from_np(a.dtype),
                                   kind="ExternalInput").ap())
    out = nc.dram_tensor("out_0", (N, D), F32, kind="ExternalOutput").ap()
    graph_network(nc, *args, out)
    r = run_bass_kernel_spmd(nc, [arrays], core_ids=[0])
    return r.results[0]["out_0"]
```

```python
from contextlib import ExitStack
import math

import concourse.bass as bass
from concourse import mybir

ALU = mybir.AluOpType
ACT = mybir.ActivationFunctionType
F32 = mybir.dt.float32
F16 = mybir.dt.float16
BF16 = mybir.dt.bfloat16
I32 = mybir.dt.int32
AX_X = mybir.AxisListType.X

P = 128
N = 8192
D = 256
NB = N // P
GROUP = 1024
TILES = GROUP // P
STEPS = N // GROUP
LOAD = 2048
LOADS = N // LOAD
SLOTS = 3
RING = 4
QUARTERS = 4
QUARTER = NB // QUARTERS
EPS = 1e-5
MASKED = -(2.0 ** 100)
EXP_SHIFT = 15.0 * math.log(2.0)
EARLY = 2
X_TOP = 2.0 ** 14
ROW = D + 4


def value(r, off):
    return SLOTS * r + off


def ahead(off, t, k, steps):
    more, k = divmod(k + steps, STEPS)
    return off + more, does(t, more), k


def does(t, lag):
    return t is None or 0 <= t + lag < NB


def graph_network(nc, x, adj, h_v, w, out):
    scores_row = nc.dram_tensor("scores_row", (NB, P), F32).ap()
    y_rows = nc.dram_tensor("y_rows", (N, ROW), F32).ap()
    x1_rows = nc.dram_tensor("x1_rows", (N, ROW), F32).ap()

    with ExitStack() as ctx:
        ident = ctx.enter_context(nc.sbuf_tensor("ident", [P, P], F32))
        least_sum = ctx.enter_context(nc.sbuf_tensor("least_sum", [P, 1], F32))
        attention_layer(nc, x, adj, h_v, scores_row, y_rows, ident, least_sum)
        convolution_layer(nc, adj, w, y_rows, x1_rows, out, ident, least_sum)


def attention_layer(nc, x, adj, h_v, scores_row, y_rows, ident, least_sum):
    MARK_AHEAD, SUM_AHEAD, SCALE_AHEAD, MASK_AHEAD = 18, 17, 16, 15
    EXP_AHEAD, PARTS_AHEAD, DMA_AHEAD, PE_AHEAD = 6, 4, 3, 2
    MARKS = 3
    HIGH_BY_DVE = [7]
    LOW_BY_DVE = [3, 7]
    with ExitStack() as ctx:
        def sb(name, shape, dt):
            return ctx.enter_context(nc.sbuf_tensor(name, shape, dt))

        def sem(name):
            return ctx.enter_context(nc.semaphore(name))

        x_parts = sb("x_parts", [P, NB, 2, D], F16)
        scores = sb("scores", [P, N], F32)
        logits = sb("logits", [P, SLOTS, N], F32)
        absent = sb("absent", [P, MARKS, GROUP], BF16)
        high = sb("high", [P, 2, GROUP], F16)
        wT_hi = sb("wT_hi", [P, RING, GROUP], F16)
        wT_lo = sb("wT_lo", [P, RING, GROUP], F16)
        y = sb("y", [P, SLOTS, ROW], F32)
        step_max = sb("step_max", [P, SLOTS, STEPS], F32)
        step_exp_sum = sb("step_exp_sum", [P, SLOTS, STEPS], F32)
        step_adj_sum = sb("step_adj_sum", [P, SLOTS, STEPS], F32)
        row_max = sb("row_max", [P, SLOTS], F32)
        exp_bias = sb("exp_bias", [P, SLOTS], F32)
        present = sb("present", [P, SLOTS], F32)
        adj_sum = sb("adj_sum", [P, SLOTS], F32)
        exp_sum = sb("exp_sum", [P, SLOTS], F32)
        exp_inv = sb("exp_inv", [P, SLOTS], F32)
        factor = sb("factor", [P, SLOTS], F32)
        carrier = sb("carrier", [P, STEPS], F32)
        tail_carrier = sb("tail_carrier", [P, 1], F32)
        stats = sb("stats", [P, 6], F32)
        mean_var = sb("mean_var", [P, 2], F32)

        x_all = logits[:, 1:3, :].rearrange("p a (t d) -> p (a t) d", d=D)
        early = wT_lo[:, :, :].rearrange("p a j -> p (a j)").bitcast(F32)
        h_row = early[:, 0:D]
        score_cols = early[:, D:D + NB]
        score_rows = early[0:NB, 2 * D:2 * D + P]
        ones = early[0:1, 3 * D:3 * D + P]
        squares = sb("squares", [P, QUARTERS], F32)
        top = sb("top", [P, 1], F32)
        small = sb("small", [1, 8], F32)
        gains = sb("gains", [P, 2], F32)

        turned = [ctx.enter_context(nc.psum_tensor(f"turned{i}", [P, GROUP], F32)) for i in range(2)]
        acc = [ctx.enter_context(nc.psum_tensor(f"acc{i}", [P, 2 * D], F32)) for i in range(SLOTS)]
        scores_turned, top_turned, spread = acc[1], acc[2][:, 0:P], acc[2][:, P:P + 2]

        h_in = sem("h_in")
        x_in = [sem(f"x_in{i}") for i in range(QUARTERS)]
        ident_zero = sem("ident_zero")
        ident_ready = sem("ident_ready")
        scored = sem("scored")
        scores_turn = sem("scores_turn")
        score_rows_ready = sem("score_rows_ready")
        scores_out = sem("scores_out")
        scores_in = [sem(f"scores_in{i}") for i in range(LOADS)]
        squared = sem("squared")
        topped = sem("topped")
        top_turn = sem("top_turn")
        bound_ready = sem("bound_ready")
        rooted = sem("rooted_bound")
        chain = sem("prepare_chain")
        gain_pair = sem("gain_pair")
        gain_spread = sem("gain_spread")
        gains_ready = sem("gains_ready")
        x_high = sem("x_high")
        x_low = sem("x_low")

        loaded = [sem(f"loaded{i}") for i in range(SLOTS * LOADS)]
        x_loaded = [sem(f"x_loaded{i}") for i in range(SLOTS)]
        marked = sem("marked")
        adj_summed = sem("adj_summed")
        scaled = sem("scaled")
        masked = sem("masked")
        max_found = sem("max_found")
        bias_ready = sem("bias_ready")
        exp_done = sem("exp_done")
        high_by_act = sem("high_by_act")
        high_by_dve = sem("high_by_dve")
        low_by_pool = sem("low_by_pool")
        low_by_dve = sem("low_by_dve")
        dma_turned = [sem(f"dma_turned{i}") for i in range(RING)]
        carried = sem("carried")
        pe_turned = sem("pe_turned")
        hi_ready = sem("hi_ready")
        lo_ready = sem("lo_ready")
        multiplied = sem("multiplied")
        least_started = sem("least_started")
        tail = sem("tail")
        slots_free = sem("slots_free")
        y_ready = sem("y_ready")
        y_stored = sem("y_stored")
        y_free = sem("y_free")

        X_PARTS = [(-3, 7), (-2, 1), (-2, 2), (-2, 4)]
        TAIL_STEPS = 7
        TAIL_FROM = 2
        PAIRS = STEPS // 2
        HIGH_BY_ACT = [k for k in range(1, STEPS, 2) if k not in HIGH_BY_DVE]
        LOW_BY_POOL = [k for k in range(1, STEPS, 2) if k not in LOW_BY_DVE]

        def periods(eng, period):
            for t in (-3, -2, -1, 0):
                period(0, t, t)
            with eng.Fori(0, 20) as r:
                for off in (1, 2, 3):
                    period(r, off, None)
            for t in (61, 62, 63, 64):
                period(0, t, t)

        def static_below(r, g, n):
            return isinstance(r, int) and g < n

        def await_dma_turned(eng, r, off, k):
            eng.wait_ge(dma_turned[k % RING], 32 * (2 * value(r, off) + k // RING + 1))

        def mark_place(off, k):
            return (off * STEPS + k) % MARKS

        def low_place(off, k):
            return logits[:, off % SLOTS, k * GROUP:k * GROUP + GROUP // 2].bitcast(F16)

        def await_part(eng, by_dve, dve_steps, by_other, other_steps, r, off, k):
            ready, steps = (by_dve, dve_steps) if k in dve_steps else (by_other, other_steps)
            eng.wait_ge(ready, len(steps) * value(r, off) + steps.index(k) + 1)

        def make_high(eng, r, off, k):
            n = PAIRS * value(r, off) + k // 2
            if not static_below(r, n, 2):
                await_dma_turned(eng, r, off + (k - 4) // STEPS, (k - 4) % STEPS)
            eng.wait_ge(exp_done, STEPS * value(r, off) + k + 1)
            return (high[:, k // 2 % 2, :], logits[:, off % SLOTS, k * GROUP:(k + 1) * GROUP])

        def subtract_high(eng, r, off, k):
            await_part(eng, high_by_dve, HIGH_BY_DVE, high_by_act, HIGH_BY_ACT, r, off, k)
            return eng.tensor_tensor(low_place(off, k),
                                     logits[:, off % SLOTS, k * GROUP:(k + 1) * GROUP],
                                     high[:, k // 2 % 2, :], ALU.subtract)

        block = ctx.enter_context(nc.Block())

        @block.sync
        def _(sp):
            sp.sem_inc(y_free, SLOTS)

            def load(r, off, c):
                sp.dma_start(logits[:, off % SLOTS, c * LOAD:(c + 1) * LOAD],
                             adj[bass.ds(value(r, off) * P, P), c * LOAD:(c + 1) * LOAD]
                             ).then_inc(loaded[(off % SLOTS) * LOADS + c], 16)

            def prepare():
                sp.dma_start(h_row, h_v.rearrange("d a -> a d").to_broadcast((P, D))
                             ).then_inc(h_in, 16)
                view = x.rearrange("(t p) d -> p t d", p=P)
                for q in range(QUARTERS):
                    rows = slice(q * QUARTER, (q + 1) * QUARTER)
                    sp.dma_start(x_all[:, rows, :], view[:, rows, :]).then_inc(x_in[q], 16)
                for c in range(LOADS):
                    load(0, 0, c)
                sp.wait_ge(score_rows_ready, 1)
                sp.dma_start(scores_row, score_rows).then_inc(scores_out, 16)
                sp.wait_ge(scores_out, 16)
                flat = scores_row.rearrange("(a t) p -> a (t p)", a=1)
                for c in range(LOADS):
                    cols = slice(c * LOAD, (c + 1) * LOAD)
                    sp.dma_start(scores[:, cols], flat[:, cols].to_broadcast((P, LOAD))
                                 ).then_inc(scores_in[c], 16)
                for q in range(QUARTERS):
                    sp.wait_ge(x_low, q + 1)
                    for c in range(2):
                        load(0, 1 + q // 2, q % 2 * 2 + c)

            def store(r, off):
                sp.wait_ge(y_ready, value(r, off) + 1)
                sp.sem_inc(carried, 1)
                sp.dma_start(y_rows[bass.ds(value(r, off) * P, P), :],
                             y[:, off % SLOTS, :]).then_inc(y_stored, 16)

            def turn(r, off, k):
                await_part(sp, low_by_dve, LOW_BY_DVE, low_by_pool, LOW_BY_POOL, r, off, k)
                sp.sem_inc(carried, 1)
                g = STEPS * value(r, off) + k
                if not static_below(r, g, RING):
                    sp.wait_ge(multiplied, g - RING + 1)
                    sp.sem_inc(carried, 1)
                for to, of in ((wT_hi, high[:, k // 2 % 2, :]), (wT_lo, low_place(off, k))):
                    sp.dma_start_transpose(to[:, k % RING, :].rearrange("p (t i) -> p t i", i=P), of
                                           ).then_inc(dma_turned[k % RING], 16)

            def period(r, off, t):
                if t == -3:
                    prepare()
                for k in range(STEPS):
                    o, there, kk = ahead(off, t, k, DMA_AHEAD)
                    if there and kk % 2 == 1:
                        turn(r, o, kk)
                    if k == 1 and does(t, 0):
                        sp.wait_ge(y_free, value(r, off) + 1)
                        sp.sem_inc(carried, 1)
                        sp.dma_start(y[:, off % SLOTS, 0:D], x[bass.ds(value(r, off) * P, P), :]
                                     ).then_inc(x_loaded[off % SLOTS], 16)
                    if k % 2 == 0 and does(t, 0) and does(t, SLOTS):
                        sp.wait_ge(pe_turned, PAIRS * value(r, off) + k // 2 + 1)
                        sp.sem_inc(carried, 1)
                        await_dma_turned(sp, r, off, k + 1)
                        sp.sem_inc(carried, 1)
                        sp.wait_ge(adj_summed, STEPS * value(r, off) + k + SUM_AHEAD + 1)
                        sp.sem_inc(carried, 1)
                        load(r, off + SLOTS, k // 2)
                    if k == 7 and does(t, -1):
                        store(r, off - 1)
                if does(t, -1):
                    sp.wait_ge(y_stored, 16 * value(r, off))
                    sp.sem_inc(y_free, 1)

            periods(sp, period)

        @block.gpsimd
        def _(pool):
            pool.memset(ident[:, :], 0.0).then_inc(ident_zero, 1)
            pool.wait_ge(ident_zero, 1)
            pool.affine_select(out=ident[:, :], in_=ident[:, :], compare_op=ALU.not_equal, fill=1.0,
                               base=0, pattern=[[-1, P]], channel_multiplier=1).then_inc(ident_ready, 1)

            def period(r, off, t):
                for k in range(STEPS):
                    o, there, _ = ahead(off, t, k, SCALE_AHEAD)
                    if there:
                        part = logits[:, o % SLOTS, k * GROUP:(k + 1) * GROUP]
                        if t == -2 and k % 2 == 0:
                            pool.wait_ge(scores_in[k // 2], 16)
                        pool.wait_ge(marked, STEPS * value(r, o) + k + 1)
                        pool.wait_ge(adj_summed, STEPS * value(r, o) + k + 1)
                        pool.tensor_tensor(part, part, scores[:, k * GROUP:(k + 1) * GROUP],
                                           ALU.mult).then_inc(scaled, 1)
                    o, there, kk = ahead(off, t, k, PARTS_AHEAD)
                    if there and kk in LOW_BY_POOL:
                        subtract_high(pool, r, o, kk).then_inc(low_by_pool, 1)

            periods(pool, period)

        @block.scalar
        def _(act):
            for q in range(QUARTERS):
                act.wait_ge(x_in[q], 16)
                rows = slice(q * QUARTER, (q + 1) * QUARTER)
                act.activation(x_parts[:, rows, 0, :], x_all[:, rows, :], ACT.Square,
                               accum_out=squares[:, q:q + 1]).then_inc(squared, 1)
            act.wait_ge(bound_ready, 1)
            act.activation(small[:, 2:3], small[:, 1:2], ACT.Sqrt).then_inc(rooted, 1)

            def x_high_part(q):
                rows = slice(q * QUARTER, (q + 1) * QUARTER)
                if q == 0:
                    act.wait_ge(gains_ready, 1)
                act.activation(x_parts[:, rows, 0, :], x_all[:, rows, :], ACT.Copy,
                               scale=gains[:, 0:1]).then_inc(x_high, 1)

            def unused_place(r, off, t, k):
                o, there, kk = ahead(off, t, k, 2 - (k + 1) % 2)
                if not there:
                    return wT_hi[:, RING - 1, :].bitcast(BF16)
                await_part(act, low_by_dve, LOW_BY_DVE, low_by_pool, LOW_BY_POOL, r, o, kk)
                return logits[:, o % SLOTS, kk * GROUP + GROUP // 2:(kk + 1) * GROUP].bitcast(BF16)

            def sum_adj(r, off, k, unused):
                u, g = off % SLOTS, STEPS * value(r, off) + k
                if k % 2 == 0:
                    act.wait_ge(loaded[u * LOADS + k // 2], 16 * (r + off // SLOTS + 1))
                if not static_below(r, g, 1):
                    act.wait_ge(adj_summed, g)
                act.activation(unused, logits[:, u, k * GROUP:(k + 1) * GROUP], ACT.Identity,
                               accum_out=step_adj_sum[:, u, k:k + 1]).then_inc(adj_summed, 1)

            def exponentiate(r, off, k):
                u = off % SLOTS
                part = logits[:, u, k * GROUP:(k + 1) * GROUP]
                if k == 0:
                    act.wait_ge(bias_ready, value(r, off) + 1)
                    act.wait_ge(slots_free, value(r, off) + 1)
                act.activation(part, part, ACT.Exp, bias=exp_bias[:, u:u + 1],
                               accum_out=step_exp_sum[:, u, k:k + 1]).then_inc(exp_done, 1)

            def high_from_psum(r, off, k):
                g = STEPS * value(r, off) + k
                act.wait_ge(pe_turned, PAIRS * value(r, off) + k // 2 + 1)
                if not static_below(r, g, RING):
                    act.wait_ge(multiplied, g - RING + 1)
                act.activation(wT_hi[:, k % RING, :], turned[k // 2 % 2][:, :],
                               ACT.Copy).then_inc(hi_ready, 1)

            def period(r, off, t):
                for k in range(STEPS):
                    o, there, kk = ahead(off, t, k, SUM_AHEAD)
                    if there:
                        sum_adj(r, o, kk, unused_place(r, off, t, k))
                    if (t, k) in X_PARTS:
                        x_high_part(X_PARTS.index((t, k)))
                    o, there, kk = ahead(off, t, k, PE_AHEAD)
                    if there and kk % 2 == 0:
                        high_from_psum(r, o, kk)
                    o, there, kk = ahead(off, t, k, PARTS_AHEAD)
                    if there and kk in HIGH_BY_ACT:
                        to, of = make_high(act, r, o, kk)
                        act.activation(to, of, ACT.Copy).then_inc(high_by_act, 1)
                    o, there, kk = ahead(off, t, k, EXP_AHEAD)
                    if there:
                        exponentiate(r, o, kk)

            periods(act, period)

        @block.vector
        def _(dve):
            dve.sem_inc(slots_free, SLOTS)
            dve.memset(least_sum[:, :], 3.0e38).then_inc(least_started, 1)
            dve.memset(ones, 1.0)
            links = [0]

            def then(ins):
                links[0] += 1
                ins.then_inc(chain, 1)
                dve.wait_ge(chain, links[0])

            dve.wait_ge(h_in, 16)
            for t in range(NB):
                if t % QUARTER == 0:
                    dve.wait_ge(x_in[t // QUARTER], 16)
                if t >= 2:
                    dve.wait_ge(scored, t - 1)
                dve.tensor_tensor_reduce(high[:, t % 2, 0:D], x_all[:, t, :], h_row, 1.0, 0.0,
                                         ALU.mult, ALU.add, score_cols[:, t:t + 1]
                                         ).then_inc(scored, 1)
            dve.wait_ge(squared, QUARTERS)
            dve.tensor_reduce(top[:, :], squares[:, :], AX_X, ALU.max).then_inc(topped, 1)
            dve.wait_ge(scores_turn, 1)
            dve.tensor_copy(score_rows, scores_turned[0:NB, 0:P]).then_inc(score_rows_ready, 1)
            dve.wait_ge(top_turn, 1)
            then(dve.tensor_reduce(small[:, 0:1], top_turned[0:1, :], AX_X, ALU.max))
            dve.tensor_scalar(small[:, 1:2], small[:, 0:1], 2.0 ** -100, None, ALU.max
                              ).then_inc(bound_ready, 1)
            dve.wait_ge(rooted, 1)
            then(dve.tensor_scalar(small[:, 3:4].bitcast(I32), small[:, 2:3].bitcast(I32),
                                   0x7F800000, None, ALU.bitwise_and))
            then(dve.reciprocal(small[:, 4:5], small[:, 3:4]))
            dve.tensor_scalar(small[:, 7:8], small[:, 3:4], 1.0 / X_TOP, None, ALU.mult)
            dve.tensor_scalar(small[:, 6:7], small[:, 4:5], X_TOP, None, ALU.mult
                              ).then_inc(gain_pair, 1)
            dve.wait_ge(gain_spread, 1)
            dve.tensor_copy(gains[:, :], spread).then_inc(gains_ready, 1)
            dve.wait_ge(gains_ready, 1)

            def x_low_part(q):
                dve.wait_ge(x_high, q + 1)
                rows = slice(q * QUARTER, (q + 1) * QUARTER)
                dve.scalar_tensor_tensor(out=x_parts[:, rows, 1, :], in0=x_all[:, rows, :],
                                         scalar=gains[:, 0:1], in1=x_parts[:, rows, 0, :],
                                         op0=ALU.mult, op1=ALU.subtract).then_inc(x_low, 1)

            def mark(r, off, k):
                u, g = off % SLOTS, STEPS * value(r, off) + k
                if k % 2 == 0:
                    dve.wait_ge(loaded[u * LOADS + k // 2], 16 * (r + off // SLOTS + 1))
                if not static_below(r, g, MARKS):
                    dve.wait_ge(masked, g - MARKS + 1)
                dve.tensor_scalar(absent[:, mark_place(off, k), :], logits[:, u, k * GROUP:(k + 1) * GROUP],
                                  0.0, MASKED, ALU.is_equal, ALU.mult).then_inc(marked, 1)

            def mask(r, off, k):
                u, g = off % SLOTS, STEPS * value(r, off) + k
                part = logits[:, u, k * GROUP:(k + 1) * GROUP]
                dve.wait_ge(marked, g + 1)
                dve.wait_ge(scaled, g + 1)
                dve.memset(carrier[:, k:k + 1], 0.0)
                dve.tensor_tensor_reduce(part, part, absent[:, mark_place(off, k), :], 1.0, 2 * MASKED,
                                         ALU.add, ALU.max,
                                         step_max[:, u, k:k + 1]).then_inc(masked, 1)

            def finish_max(r, off):
                u, b = off % SLOTS, value(r, off)
                dve.wait_ge(masked, STEPS * b + STEPS)
                dve.tensor_reduce(row_max[:, u:u + 1], step_max[:, u, :], AX_X,
                                  ALU.max).then_inc(max_found, 1)
                dve.wait_ge(adj_summed, STEPS * b + STEPS)
                dve.tensor_reduce(adj_sum[:, u:u + 1], step_adj_sum[:, u, :], AX_X, ALU.add)
                dve.wait_ge(max_found, b + 1)
                dve.tensor_scalar(present[:, u:u + 1], row_max[:, u:u + 1], MASKED / 2,
                                  gains[:, 1:2], ALU.is_gt, ALU.mult)
                dve.tensor_scalar(exp_bias[:, u:u + 1], row_max[:, u:u + 1], -1.0, EXP_SHIFT,
                                  ALU.mult, ALU.add).then_inc(bias_ready, 1)

            def low_from_psum(r, off, k):
                dve.wait_ge(hi_ready, PAIRS * value(r, off) + k // 2 + 1)
                dve.tensor_tensor(wT_lo[:, k % RING, :], turned[k // 2 % 2][:, :],
                                  wT_hi[:, k % RING, :], ALU.subtract).then_inc(lo_ready, 1)

            def finish_block(r, off, n):
                u, b = off % SLOTS, value(r, off)
                if n:
                    dve.wait_ge(tail, TAIL_STEPS * b + n)
                if n == 0:
                    dve.wait_ge(exp_done, STEPS * b + STEPS)
                    dve.wait_ge(bias_ready, b + 1)
                    dve.tensor_reduce(exp_sum[:, u:u + 1], step_exp_sum[:, u, :], AX_X,
                                      ALU.add).then_inc(tail, 1)
                elif n == 1:
                    dve.reciprocal(exp_inv[:, u:u + 1], exp_sum[:, u:u + 1]).then_inc(tail, 1)
                    dve.wait_ge(x_loaded[u], 16 * (r + off // SLOTS + 1))
                    dve.tensor_scalar(y[:, u, D:D + 1], adj_sum[:, u:u + 1], 1.0, None, ALU.add)
                    dve.tensor_tensor(least_sum[:, :], least_sum[:, :], adj_sum[:, u:u + 1],
                                      ALU.min)
                elif n == 2:
                    dve.tensor_tensor(factor[:, u:u + 1], exp_inv[:, u:u + 1],
                                      present[:, u:u + 1], ALU.mult).then_inc(tail, 1)
                elif n == 3:
                    dve.wait_ge(multiplied, STEPS * b + STEPS)
                    dve.scalar_tensor_tensor(out=y[:, u, 0:D], in0=acc[u][:, D:2 * D],
                                             scalar=factor[:, u:u + 1], in1=y[:, u, 0:D],
                                             op0=ALU.mult, op1=ALU.add).then_inc(tail, 1)
                elif n == 4:
                    dve.scalar_tensor_tensor(out=y[:, u, 0:D], in0=acc[u][:, 0:D],
                                             scalar=factor[:, u:u + 1], in1=y[:, u, 0:D],
                                             op0=ALU.mult, op1=ALU.add).then_inc(tail, 1)
                elif n == 5:
                    dve.bn_stats(stats[:, :], y[:, u, 0:D]).then_inc(tail, 1)
                    dve.memset(y[:, u, D + 3:D + 4], 0.0)
                elif n == 6:
                    dve.memset(tail_carrier[:, :], 0.0)
                    dve.bn_aggr(mean_var[:, :], stats[:, :]).then_inc(tail, 1)
                else:
                    dve.tensor_scalar(y[:, u, D + 1:D + 2], mean_var[:, 1:2], EPS, None, ALU.add)
                    dve.tensor_copy(y[:, u, D + 2:D + 3], mean_var[:, 0:1]).then_inc(y_ready, 1)
                    dve.sem_inc(slots_free, 1)

            def period(r, off, t):
                for k in range(STEPS):
                    if (t, k) in X_PARTS:
                        x_low_part(X_PARTS.index((t, k)))
                    o, there, kk = ahead(off, t, k, MASK_AHEAD)
                    if there:
                        mask(r, o, kk)
                        if kk == STEPS - 1:
                            finish_max(r, o)
                    if TAIL_FROM <= k < TAIL_FROM + 4 and does(t, -1):
                        finish_block(r, off - 1, 2 * (k - TAIL_FROM))
                    o, there, kk = ahead(off, t, k, MARK_AHEAD)
                    if there:
                        mark(r, o, kk)
                    o, there, kk = ahead(off, t, k, PE_AHEAD)
                    if there and kk % 2 == 0:
                        low_from_psum(r, o, kk)
                    o, there, kk = ahead(off, t, k, PARTS_AHEAD)
                    if there and kk in HIGH_BY_DVE:
                        to, of = make_high(dve, r, o, kk)
                        dve.tensor_copy(to, of).then_inc(high_by_dve, 1)
                    if TAIL_FROM <= k < TAIL_FROM + 4 and does(t, -1):
                        finish_block(r, off - 1, 2 * (k - TAIL_FROM) + 1)
                    if there and kk in LOW_BY_DVE:
                        subtract_high(dve, r, o, kk).then_inc(low_by_dve, 1)

            periods(dve, period)

        @block.tensor
        def _(pe):
            pe.wait_ge(ident_ready, 1)
            pe.wait_ge(scored, NB)
            pe.transpose(scores_turned[0:NB, 0:P], score_cols, ident[:, :]
                         ).then_inc(scores_turn, 1)
            pe.wait_ge(topped, 1)
            pe.transpose(top_turned[0:1, :], top[:, 0:1], ident[:, :]).then_inc(top_turn, 1)
            pe.wait_ge(gain_pair, 1)
            pe.matmul(spread, ones, small[:, 6:8], start=True, stop=True
                      ).then_inc(gain_spread, 1)

            def turn(r, off, k):
                m = PAIRS * value(r, off) + k // 2
                pe.wait_ge(exp_done, STEPS * value(r, off) + k + 1)
                if not static_below(r, m, 2):
                    pe.wait_ge(lo_ready, m - 1)
                for i in range(TILES):
                    at = k * GROUP + i * P
                    mm = pe.transpose(turned[k // 2 % 2][:, i * P:(i + 1) * P],
                                      logits[:, off % SLOTS, at:at + P], ident[:, :])
                mm.then_inc(pe_turned, 1)

            def period(r, off, t):
                if does(t, 0):
                    if t == 0:
                        pe.wait_ge(x_low, QUARTERS)
                    pe.wait_ge(slots_free, value(r, off) + 1)
                for k in range(STEPS):
                    o, there, kk = ahead(off, t, k, PE_AHEAD)
                    if there and kk % 2 == 0:
                        turn(r, o, kk)
                    if not does(t, 0):
                        continue
                    if k % 2 == 0:
                        pe.wait_ge(lo_ready, PAIRS * value(r, off) + k // 2 + 1)
                    else:
                        await_dma_turned(pe, r, off, k)
                    for i in range(TILES):
                        j = k * TILES + i
                        tile = slice(i * P, (i + 1) * P)
                        pe.matmul(acc[off % SLOTS][:, :], wT_hi[:, k % RING, tile],
                                  x_parts[:, j, :, :].rearrange("p a d -> p (a d)"),
                                  start=(j == 0), stop=(j == NB - 1), skip_group_check=True)
                        mm = pe.matmul(acc[off % SLOTS][:, D:2 * D], wT_lo[:, k % RING, tile],
                                       x_parts[:, j, 0, :], start=False, stop=(j == NB - 1),
                                       skip_group_check=True)
                    mm.then_inc(multiplied, 1)

            periods(pe, period)


def convolution_layer(nc, adj, w, y_rows, x1_rows, out, ident, least_sum):
    with ExitStack() as ctx:
        def sb(name, shape, dt):
            return ctx.enter_context(nc.sbuf_tensor(name, shape, dt))

        support = sb("support", [P, NB, 2, D], F16)
        rows = sb("rows", [P, SLOTS, N], F32)
        step_top = sb("step_top", [P, SLOTS, STEPS], F32)
        prepare_support(nc, adj, w, y_rows, x1_rows, ident, least_sum, support, rows, step_top)
        aggregate(nc, adj, x1_rows, out, ident, support, rows, step_top)


def prepare_support(nc, adj, w, y_rows, x1_rows, ident, least_sum, support, rows, step_top):
    BUFS = 4
    PAIR = 2
    PAIRS = NB // PAIR
    LOOPS = 5
    LAST = 3 + LOOPS * BUFS
    LATE = LOOPS * GROUP
    with ExitStack() as ctx:
        def sb(name, shape, dt):
            return ctx.enter_context(nc.sbuf_tensor(name, shape, dt))

        def sem(name):
            return ctx.enter_context(nc.semaphore(name))

        w_in = sb("w_in", [P, 2, D], F32)
        w_square = sb("w_square", [P, 2, D], F32)
        w_norms = sb("w_norms", [P, 2], F32)
        extremes = sb("extremes", [P, 2], F32)
        small = sb("small1", [1, 8], F32)
        ones = sb("ones1", [1, P], F32)
        gains = sb("gains1", [P, 2], F32)
        wT = sb("wT", [P, 2, D], F32)
        y = sb("y_again", [P, BUFS, PAIR, ROW], F32)
        root = sb("root", [P, BUFS, PAIR, 2], F32)
        dinv = sb("dinv", [P, BUFS, PAIR, 2], F32)
        x1 = sb("x1", [P, BUFS, PAIR, ROW], F32)
        shift = sb("shift", [P, BUFS], F32)
        x1T = sb("x1T", [P, BUFS, PAIR * D], F32)
        w_turned = ctx.enter_context(nc.psum_tensor("w_turned", [P, 2 * D], F32))
        extremes_turned = ctx.enter_context(nc.psum_tensor("extremes_turned", [P, 512], F32))
        spread = extremes_turned[:, 2 * P:2 * P + 2]
        turned = [ctx.enter_context(nc.psum_tensor(f"x1_turned{i}", [P, PAIR * D], F32))
                  for i in range(2)]
        product = [ctx.enter_context(nc.psum_tensor(f"product{i}", [P, PAIR * D], F32))
                   for i in range(BUFS)]

        w_loaded = sem("w_loaded")
        w_turn = sem("w_turn")
        w_ready = sem("w_ready")
        chain = sem("gain_chain")
        extremes_ready = sem("extremes_ready")
        extremes_turn = sem("extremes_turn")
        bound_squared = sem("bound_squared")
        bound_ready = sem("bound_ready")
        gain_pair = sem("gain_pair1")
        gain_spread = sem("gain_spread1")
        gains_ready = sem("gains_ready")
        loaded = [sem(f"y_loaded{i}") for i in range(BUFS)]
        fetched = [sem(f"fetched{i}") for i in range(EARLY)]
        rooted = sem("rooted")
        inverted = sem("inverted")
        shift_ready = sem("shift_ready")
        x1_by_dve = sem("x1_by_dve")
        x1_by_act = sem("x1_by_act")
        factors_ready = sem("factors_ready")
        x1_stored = [sem(f"x1_stored{i}") for i in range(BUFS)]
        turn_done = sem("turn_done")
        x1T_ready = sem("x1T_ready")
        product_done = sem("product_done")
        support_hi = sem("support_hi")
        support_lo = sem("support_lo")

        def periods(eng, period, before={}):
            for t in (-3, -2, -1, 0, 1, 2):
                if t in before:
                    before[t]()
                period(0, t, t)
            with eng.Fori(0, LOOPS) as r:
                for off in (3, 4, 5, 6):
                    period(r, off, None)
            for t in range(LAST, PAIRS + 1):
                period(0, t, t)

        def has(t, lag):
            return t is None or 0 <= t + lag < PAIRS

        def pair_of(dram, m):
            return dram[bass.ds(m * PAIR * P, PAIR * P), :].rearrange("(a p) d -> p a d", p=P)

        def await_x1_place(eng, r, off, t):
            if t is None or t + 2 >= BUFS:
                done = BUFS * r + off + 2 - BUFS + 1
                eng.wait_ge(x1_stored[(off + 2) % BUFS], 16 * (r + (off + 2) // BUFS))
                eng.wait_ge(turn_done, done)
                eng.wait_ge(support_lo, done)

        def support_part(m, a, part):
            return support[:, bass.ds(m * PAIR + a, 1), part, :].rearrange("p a d -> p (a d)")

        block = ctx.enter_context(nc.Block())

        @block.sync
        def _(sp):
            sp.dma_start(w_in[:, :, :], w.rearrange("(a p) d -> p a d", p=P)).then_inc(w_loaded, 16)

            def load(r, off):
                sp.dma_start(y[:, off % BUFS, :, :], pair_of(y_rows, BUFS * r + off)
                             ).then_inc(loaded[off % BUFS], 16)

            def period(r, off, t):
                m = BUFS * r + off
                if t == -3:
                    for b in range(BUFS):
                        load(0, b)
                if has(t, 2):
                    u = (off + 2) % BUFS
                    sp.wait_ge(x1_by_dve, m + 3)
                    sp.wait_ge(x1_by_act, m + 3)
                    if has(t, 2 + BUFS):
                        load(r, off + 2 + BUFS)
                    sp.wait_ge(factors_ready, m + 3)
                    sp.dma_start(pair_of(x1_rows, m + 2), x1[:, u, :, :]
                                 ).then_inc(x1_stored[u], 16)
                if t is None and off - 3 < EARLY:
                    i = off - 3
                    sp.dma_start(rows[:, i, bass.ds(r * GROUP, GROUP)],
                                 adj[i * P:(i + 1) * P, bass.ds(r * GROUP, GROUP)]
                                 ).then_inc(fetched[i], 16)
                if t in (LAST, LAST + 3):
                    i = (t - LAST) // 3
                    sp.dma_start(rows[:, i, LATE:], adj[i * P:(i + 1) * P, LATE:]
                                 ).then_inc(fetched[i], 16)

            periods(sp, period)
            for i in range(BUFS):
                sp.wait_ge(x1_stored[i], 16 * (PAIRS // BUFS))

        @block.scalar
        def _(act):
            def root_of_bound():
                act.wait_ge(bound_squared, 1)
                act.activation(small[:, 3:4], small[:, 2:3], ACT.Sqrt).then_inc(bound_ready, 1)

            def period(r, off, t):
                m = BUFS * r + off
                if has(t, 3):
                    u = (off + 3) % BUFS
                    act.wait_ge(loaded[u], 16 * (r + (off + 3) // BUFS + 1))
                    if t is None or t + 3 >= BUFS:
                        act.wait_ge(inverted, m + 3 - BUFS + 1)
                    act.activation(root[:, u, :, :], y[:, u, :, D:D + 2], ACT.Sqrt
                                   ).then_inc(rooted, 1)
                if has(t, -1):
                    act.wait_ge(product_done, m)
                    act.wait_ge(factors_ready, m)
                    for a in range(PAIR):
                        ins = act.activation(support_part(m - 1, a, 0),
                                             product[(off - 1) % BUFS][:, a * D:(a + 1) * D],
                                             ACT.Copy, scale=x1[:, (off - 1) % BUFS, a, D:D + 1])
                    ins.then_inc(support_hi, 1)
                if has(t, 1):
                    act.wait_ge(turn_done, m + 2)
                    if t is None or t + 1 >= BUFS:
                        act.wait_ge(product_done, m + 1 - BUFS + 1)
                    act.activation(x1T[:, (off + 1) % BUFS, :], turned[(off + 1) % 2][:, :],
                                   ACT.Copy).then_inc(x1T_ready, 1)
                if has(t, 2):
                    u = (off + 2) % BUFS
                    act.wait_ge(shift_ready, m + 3)
                    await_x1_place(act, r, off, t)
                    act.activation(x1[:, u, 1, 0:D], y[:, u, 1, 0:D], ACT.Identity,
                                   bias=shift[:, u:u + 1], scale=dinv[:, u, 1, 1:2]
                                   ).then_inc(x1_by_act, 1)
            periods(act, period, {0: root_of_bound})

        @block.vector
        def _(dve):
            links = [0]

            def follows(ins):
                links[0] += 1
                ins.then_inc(chain, 1)
                dve.wait_ge(chain, links[0])

            dve.memset(ones[:, :], 1.0)
            dve.memset(x1[:, :, :, D + 2:], 0.0)
            dve.tensor_scalar(extremes[:, 1:2], least_sum[:, :], 1.0, None, ALU.add).then_inc(chain, 1)
            links[0] += 1
            dve.wait_ge(w_loaded, 16)
            for i in range(2):
                ins = dve.tensor_tensor_reduce(w_square[:, i, :], w_in[:, i, :], w_in[:, i, :],
                                               1.0, 0.0, ALU.mult, ALU.add, w_norms[:, i:i + 1])
            follows(ins)
            follows(dve.reciprocal(extremes[:, 1:2], extremes[:, 1:2]))
            dve.tensor_reduce(extremes[:, 0:1], w_norms[:, :], AX_X, ALU.max
                              ).then_inc(extremes_ready, 1)

            def take_w():
                dve.wait_ge(w_turn, 1)
                dve.tensor_copy(wT[:, :, :].rearrange("p a d -> p (a d)"), w_turned[:, :]
                                ).then_inc(w_ready, 1)

            def find_gain():
                dve.wait_ge(extremes_turn, 1)
                follows(dve.tensor_reduce(small[:, 0:2], extremes_turned[0:1, 0:2 * P].rearrange(
                    "a (b p) -> a b p", b=2), AX_X, ALU.max))
                follows(dve.tensor_tensor(small[:, 2:3], small[:, 0:1], small[:, 1:2], ALU.mult))
                follows(dve.tensor_scalar(small[:, 2:3], small[:, 2:3], float(D), 2.0 ** -100,
                                          ALU.mult, ALU.max))
                dve.sem_inc(bound_squared, 1)
                dve.wait_ge(bound_ready, 1)
                follows(dve.tensor_scalar(small[:, 4:5].bitcast(I32), small[:, 3:4].bitcast(I32),
                                          0x7F800000, None, ALU.bitwise_and))
                follows(dve.reciprocal(small[:, 5:6], small[:, 4:5]))
                dve.tensor_scalar(small[:, 7:8], small[:, 4:5], 1.0 / X_TOP, None, ALU.mult)
                dve.tensor_scalar(small[:, 6:7], small[:, 5:6], X_TOP, None, ALU.mult
                                  ).then_inc(gain_pair, 1)
                dve.wait_ge(gain_spread, 1)
                dve.tensor_copy(gains[:, :], spread).then_inc(gains_ready, 1)
                dve.wait_ge(gains_ready, 1)
                for u in range(2):
                    make_factors(u)

            def make_factors(u):
                dve.tensor_scalar(x1[:, u, :, D:D + 1], dinv[:, u, :, 0:1], gains[:, 0:1], None,
                                  ALU.mult)
                dve.tensor_scalar(x1[:, u, :, D + 1:D + 2], dinv[:, u, :, 0:1], gains[:, 1:2], None,
                                  ALU.mult).then_inc(factors_ready, 1)

            def period(r, off, t):
                m = BUFS * r + off
                if has(t, 3):
                    u = (off + 3) % BUFS
                    dve.wait_ge(rooted, m + 4)
                    if t is None or t + 3 >= BUFS:
                        dve.wait_ge(factors_ready, m + 3 - BUFS + 1)
                        dve.wait_ge(x1_by_act, m + 3 - BUFS + 1)
                    dve.reciprocal(dinv[:, u, :, :], root[:, u, :, :]).then_inc(inverted, 1)
                if has(t, 2):
                    u = (off + 2) % BUFS
                    await_x1_place(dve, r, off, t)
                    dve.tensor_scalar(x1[:, u, 0, 0:D], y[:, u, 0, 0:D], y[:, u, 0, D + 2:D + 3],
                                      dinv[:, u, 0, 1:2], ALU.subtract, ALU.mult
                                      ).then_inc(x1_by_dve, 1)
                if has(t, 3):
                    u = (off + 3) % BUFS
                    dve.wait_ge(inverted, m + 4)
                    dve.tensor_scalar(shift[:, u:u + 1], y[:, u, 1, D + 2:D + 3],
                                      dinv[:, u, 1, 1:2], -1.0, ALU.mult, ALU.mult
                                      ).then_inc(shift_ready, 1)
                if has(t, 2) and (t is None or t >= 0):
                    make_factors((off + 2) % BUFS)
                if t == -2:
                    take_w()
                if has(t, -1):
                    dve.wait_ge(support_hi, m)
                    for a in range(PAIR):
                        ins = dve.scalar_tensor_tensor(
                            out=support_part(m - 1, a, 1),
                            in0=product[(off - 1) % BUFS][:, a * D:(a + 1) * D],
                            scalar=x1[:, (off - 1) % BUFS, a, D:D + 1],
                            in1=support_part(m - 1, a, 0), op0=ALU.mult, op1=ALU.subtract)
                    ins.then_inc(support_lo, 1)
                if t is None and off - 5 in range(EARLY):
                    i = off - 5
                    dve.wait_ge(fetched[i], 16 * (r + 1))
                    dve.tensor_reduce(step_top[:, i, bass.ds(r, 1)],
                                      rows[:, i, bass.ds(r * GROUP, GROUP)],
                                      AX_X, ALU.max, apply_absolute_value=True)

                if t is not None and t >= LAST + 2 and t - (LAST + 2) < EARLY * (STEPS - LOOPS):
                    i, k = divmod(t - (LAST + 2), STEPS - LOOPS)
                    k += LOOPS
                    dve.wait_ge(fetched[i], 16 * (LOOPS + 1))
                    dve.tensor_reduce(step_top[:, i, k:k + 1],
                                      rows[:, i, k * GROUP:(k + 1) * GROUP],
                                      AX_X, ALU.max, apply_absolute_value=True)

            periods(dve, period, {0: find_gain})

        @block.tensor
        def _(pe):
            pe.wait_ge(w_loaded, 16)
            for k in range(2):
                for i in range(2):
                    mm = pe.transpose(w_turned[:, k * D + i * P:k * D + (i + 1) * P],
                                      w_in[:, i, k * P:(k + 1) * P], ident[:, :])
            mm.then_inc(w_turn, 1)

            def turn_extremes():
                pe.wait_ge(extremes_ready, 1)
                for i in range(2):
                    mm = pe.transpose(extremes_turned[0:1, i * P:(i + 1) * P], extremes[:, i:i + 1],
                                      ident[:, :])
                mm.then_inc(extremes_turn, 1)
                pe.wait_ge(w_ready, 1)

            def spread_gains():
                pe.wait_ge(gain_pair, 1)
                pe.matmul(spread, ones[:, :], small[:, 6:8], start=True, stop=True
                          ).then_inc(gain_spread, 1)

            def period(r, off, t):
                m = BUFS * r + off
                if has(t, 1):
                    pe.wait_ge(x1_by_dve, m + 2)
                    pe.wait_ge(x1_by_act, m + 2)
                    if t is None or t + 1 >= 2:
                        pe.wait_ge(x1T_ready, m)
                    for a in range(PAIR):
                        for k in range(2):
                            at = a * D + k * P
                            mm = pe.transpose(turned[(off + 1) % 2][:, at:at + P],
                                              x1[:, (off + 1) % BUFS, a, k * P:(k + 1) * P],
                                              ident[:, :])
                    mm.then_inc(turn_done, 1)
                if has(t, 0):
                    pe.wait_ge(x1T_ready, m + 1)
                    if t is None or t >= BUFS:
                        pe.wait_ge(support_lo, m - BUFS + 1)
                    for a in range(PAIR):
                        for k in range(2):
                            at = a * D + k * P
                            mm = pe.matmul(product[off % BUFS][:, a * D:(a + 1) * D],
                                           x1T[:, off % BUFS, at:at + P], wT[:, k, :],
                                           start=(k == 0), stop=(k == 1))
                    mm.then_inc(product_done, 1)

            periods(pe, period, {0: turn_extremes, 1: spread_gains})


def aggregate(nc, adj, x1_rows, out, ident, support, rows, step_top):
    BY_PE = {2: 0, 4: 1, 7: 0}
    PE_ORDER = sorted(BY_PE)
    BY_DMA = [k for k in range(STEPS) if k not in BY_PE]
    PARTS_AHEAD, DMA_AHEAD, PE_AHEAD = 4, 3, 2

    with ExitStack() as ctx:
        def sb(name, shape, dt):
            return ctx.enter_context(nc.sbuf_tensor(name, shape, dt))

        def sem(name):
            return ctx.enter_context(nc.semaphore(name))

        parts = sb("parts", [P, RING, 2, GROUP], F16)
        aT = sb("aT", [P, RING, 2, GROUP], F16)
        ident16 = sb("ident16", [P, P], F16)
        top = sb("row_top", [P, SLOTS, 3], F32)
        scale = sb("scale", [P, SLOTS], F32)
        inv_scale = sb("inv_scale", [P, SLOTS], F32)
        x1 = sb("x1_again", [P, SLOTS, ROW], F32)
        own = sb("own", [P, D], F32)
        carrier = sb("carrier1", [P, 1], F32)
        total_lo = sb("total_lo", [P, D], F32)
        total = sb("total", [P, D], F32)
        message = sb("message", [P, SLOTS, D], F32)
        y = sb("y1", [P, D], F32)
        stats = sb("stats1", [P, 6], F32)
        mean_var = sb("mean_var1", [P, 2], F32)
        eps = sb("eps", [P, 1], F32)
        root = sb("root1", [P, 1], F32)
        rstd = sb("rstd1", [P, 1], F32)
        result = sb("result", [P, SLOTS, D], F32)

        turned = [ctx.enter_context(nc.psum_tensor(f"a_turned{i}", [P, 2 * GROUP], F16)) for i in range(2)]
        acc = [ctx.enter_context(nc.psum_tensor(f"a_acc{i}", [P, 2 * D], F32)) for i in range(SLOTS)]

        loaded = [sem(f"a_loaded{i}") for i in range(SLOTS * LOADS)]
        x1_loaded = [sem(f"x1_loaded{i}") for i in range(SLOTS)]
        ident16_ready = sem("ident16_ready")
        topped = sem("a_topped")
        scaling = sem("scaling")
        scale_ready = sem("scale_ready")
        hi_ready = sem("a_hi_ready")
        lo_ready = sem("a_lo_ready")
        dma_turned = [sem(f"dma_turned{i}") for i in range(RING)]
        pe_turned = sem("pe_turned")
        evacuated = sem("evacuated")
        multiplied = sem("a_multiplied")
        totalled = sem("totalled")
        message_ready = sem("message_ready")
        varied = sem("varied")
        rooted = sem("a_rooted")
        tail = sem("a_tail")
        slots_free = sem("a_slots_free")
        carried = sem("carried")
        stored = sem("stored")
        result_free = sem("result_free")

        TAIL_STEPS = 6
        SCALING_STEPS = 4

        def periods(eng, period):
            for t in (-1, 0):
                period(0, t, t)
            with eng.Fori(0, 20) as r:
                for off in (1, 2, 3):
                    period(r, off, None)
            for t in (61, 62, 63, 64):
                period(0, t, t)

        def transposed_by(eng, r, off, k):
            if k in BY_PE:
                eng.wait_ge(pe_turned, len(BY_PE) * value(r, off) + PE_ORDER.index(k) + 1)
            else:
                same = [j for j in BY_DMA if j % RING == k % RING]
                eng.wait_ge(dma_turned[k % RING],
                            16 * (len(same) * value(r, off) + same.index(k) + 1))

        block = ctx.enter_context(nc.Block())

        @block.sync
        def _(sp):
            sp.sem_inc(result_free, SLOTS)

            def load(r, off, c):
                sp.dma_start(rows[:, off % SLOTS, c * LOAD:(c + 1) * LOAD],
                             adj[bass.ds(value(r, off) * P, P), c * LOAD:(c + 1) * LOAD]
                             ).then_inc(loaded[(off % SLOTS) * LOADS + c], 16)

            def turn(r, off, k):
                g = STEPS * value(r, off) + k
                sp.wait_ge(lo_ready, g + 1)
                sp.sem_inc(carried, 1)
                if not (isinstance(r, int) and g < RING):
                    sp.wait_ge(multiplied, g - RING + 1)
                    sp.sem_inc(carried, 1)
                sp.dma_start_transpose(
                    aT[:, k % RING, :, :].rearrange("p a (t i) -> p (a t) i", i=P),
                    parts[:, k % RING, :, :].rearrange("p a j -> p (a j)")
                ).then_inc(dma_turned[k % RING], 16)

            def period(r, off, t):
                if does(t, 0):
                    sp.wait_ge(slots_free, value(r, off) + 1)
                    sp.dma_start(x1[:, off % SLOTS, :], x1_rows[bass.ds(value(r, off) * P, P), :]
                                 ).then_inc(x1_loaded[off % SLOTS], 16)
                for k in range(STEPS):
                    o, there, kk = ahead(off, t, k, DMA_AHEAD)
                    if there and kk in BY_DMA:
                        turn(r, o, kk)
                    if t == -1 and k >= STEPS - LOADS:
                        for b in range(EARLY, SLOTS):
                            load(0, b, k - (STEPS - LOADS))
                    if k % 2 == 1 and does(t, 0) and does(t, SLOTS):
                        sp.wait_ge(lo_ready, STEPS * value(r, off) + k + 1)
                        load(r, off + SLOTS, k // 2)
                    if k == 5 and does(t, -1):
                        b = value(r, off - 1)
                        sp.wait_ge(tail, TAIL_STEPS * b + TAIL_STEPS)
                        sp.dma_start(out[bass.ds(b * P, P), :], result[:, (off - 1) % SLOTS, :]
                                     ).then_inc(stored, 16)
                if does(t, -1):
                    sp.wait_ge(stored, 16 * value(r, off))
                    sp.sem_inc(result_free, 1)

            periods(sp, period)

        @block.scalar
        def _(act):
            def high_part(r, off, k):
                g = STEPS * value(r, off) + k
                u = off % SLOTS
                act.wait_ge(scale_ready, value(r, off) + 1)
                if not (isinstance(r, int) and g < RING):
                    transposed_by(act, r, off + (k - RING) // STEPS, (k - RING) % STEPS)
                act.activation(parts[:, k % RING, 0, :], rows[:, u, k * GROUP:(k + 1) * GROUP],
                               ACT.Copy, scale=scale[:, u:u + 1]).then_inc(hi_ready, 1)

            def evacuate(r, off, k):
                m = len(BY_PE) * value(r, off) + PE_ORDER.index(k)
                g = STEPS * value(r, off) + k
                act.wait_ge(pe_turned, m + 1)
                if not (isinstance(r, int) and g < RING):
                    act.wait_ge(multiplied, g - RING + 1)
                act.activation(aT[:, k % RING, :, :].rearrange("p a j -> p (a j)"),
                               turned[BY_PE[k]][:, :], ACT.Copy).then_inc(evacuated, 1)

            def period(r, off, t):
                for k in range(STEPS):
                    o, there, kk = ahead(off, t, k, PARTS_AHEAD)
                    if there:
                        high_part(r, o, kk)
                    o, there, kk = ahead(off, t, k, PE_AHEAD)
                    if there and kk in BY_PE:
                        evacuate(r, o, kk)
                    if does(t, -1) and k == 3:
                        u, b = (off - 1) % SLOTS, value(r, off - 1)
                        act.wait_ge(totalled, b + 1)
                        act.wait_ge(x1_loaded[u], 16 * (r + (off - 1) // SLOTS + 1))
                        act.activation(message[:, u, :], total[:, :], ACT.Relu,
                                       scale=x1[:, u, D + 1:D + 2]).then_inc(message_ready, 1)
                    if does(t, -1) and k == 4:
                        act.wait_ge(varied, value(r, off - 1) + 1)
                        act.activation(root[:, :], mean_var[:, 1:2], ACT.Sqrt,
                                       bias=eps[:, 0:1]).then_inc(rooted, 1)

            periods(act, period)

        @block.vector
        def _(dve):
            dve.sem_inc(slots_free, SLOTS)
            dve.tensor_copy(ident16[:, :], ident[:, :]).then_inc(ident16_ready, 1)
            dve.memset(eps[:, :], EPS)

            def find_top(r, off, k):
                u = off % SLOTS
                if k % 2 == 0:
                    dve.wait_ge(loaded[u * LOADS + k // 2],
                                16 * (r + off // SLOTS + (0 if u < EARLY else 1)))
                dve.tensor_reduce(step_top[:, u, k:k + 1], rows[:, u, k * GROUP:(k + 1) * GROUP],
                                  AX_X, ALU.max, apply_absolute_value=True).then_inc(topped, 1)

            def find_scale(r, off):
                u, b = off % SLOTS, value(r, off)

                def follows(ins, n):
                    ins.then_inc(scaling, 1)
                    dve.wait_ge(scaling, SCALING_STEPS * b + n)

                if not (isinstance(r, int) and b < EARLY):
                    dve.wait_ge(topped, STEPS * (b - EARLY + 1))
                follows(dve.tensor_reduce(top[:, u, 0:1], step_top[:, u, :], AX_X, ALU.max), 1)
                follows(dve.tensor_scalar(top[:, u, 0:1], top[:, u, 0:1], 2.0 ** -100, None,
                                          ALU.max), 2)
                follows(dve.tensor_scalar(top[:, u, 1:2].bitcast(I32), top[:, u, 0:1].bitcast(I32),
                                          0x7F800000, None, ALU.bitwise_and), 3)
                follows(dve.reciprocal(top[:, u, 2:3], top[:, u, 1:2]), 4)
                dve.tensor_scalar(inv_scale[:, u:u + 1], top[:, u, 1:2], 1.0 / X_TOP, None, ALU.mult)
                dve.tensor_scalar(scale[:, u:u + 1], top[:, u, 2:3], X_TOP, None,
                                  ALU.mult).then_inc(scale_ready, 1)

            def low_part(r, off, k):
                g = STEPS * value(r, off) + k
                u = off % SLOTS
                dve.wait_ge(hi_ready, g + 1)
                dve.scalar_tensor_tensor(out=parts[:, k % RING, 1, :],
                                         in0=rows[:, u, k * GROUP:(k + 1) * GROUP],
                                         scalar=scale[:, u:u + 1], in1=parts[:, k % RING, 0, :],
                                         op0=ALU.mult, op1=ALU.subtract).then_inc(lo_ready, 1)

            def add_parts(r, off):
                u, b = off % SLOTS, value(r, off)
                hi = support[:, bass.ds(b, 1), 0, :].rearrange("p a d -> p (a d)")
                lo = support[:, bass.ds(b, 1), 1, :].rearrange("p a d -> p (a d)")
                dve.tensor_tensor(own[:, :], hi, lo, ALU.add).then_inc(tail, 1)
                dve.wait_ge(multiplied, STEPS * b + STEPS)
                dve.wait_ge(tail, TAIL_STEPS * b + 1)
                dve.scalar_tensor_tensor(out=total_lo[:, :], in0=acc[u][:, D:2 * D],
                                         scalar=inv_scale[:, u:u + 1], in1=own[:, :],
                                         op0=ALU.mult, op1=ALU.add).then_inc(tail, 1)
                dve.wait_ge(tail, TAIL_STEPS * b + 2)
                dve.scalar_tensor_tensor(out=total[:, :], in0=acc[u][:, 0:D],
                                         scalar=inv_scale[:, u:u + 1], in1=total_lo[:, :],
                                         op0=ALU.mult, op1=ALU.add).then_inc(totalled, 1)

            def add_residual(r, off):
                u, b = off % SLOTS, value(r, off)
                dve.wait_ge(message_ready, b + 1)
                dve.tensor_tensor(y[:, :], message[:, u, :], x1[:, u, 0:D],
                                  ALU.add).then_inc(tail, 1)
                dve.wait_ge(tail, TAIL_STEPS * b + 3)
                dve.bn_stats(stats[:, :], y[:, :]).then_inc(tail, 1)
                dve.wait_ge(tail, TAIL_STEPS * b + 4)
                dve.memset(carrier[:, :], 0.0)
                dve.bn_aggr(mean_var[:, :], stats[:, :]).then_inc(varied, 1)

            def normalise(r, off):
                u, b = off % SLOTS, value(r, off)
                dve.wait_ge(rooted, b + 1)
                dve.reciprocal(rstd[:, :], root[:, :]).then_inc(tail, 1)
                dve.wait_ge(tail, TAIL_STEPS * b + 5)
                dve.wait_ge(result_free, b + 1)
                dve.tensor_scalar(result[:, u, :], y[:, :], mean_var[:, 0:1], rstd[:, 0:1],
                                  ALU.subtract, ALU.mult).then_inc(tail, 1)
                dve.sem_inc(slots_free, 1)

            def period(r, off, t):
                if t == -1:
                    find_scale(0, 0)
                for k in range(STEPS):
                    o, there, kk = ahead(off, t, k, PARTS_AHEAD)
                    if there:
                        low_part(r, o, kk)
                    if does(t, 2) and t != -1:
                        find_top(r, off + 2, k)
                    if does(t, -1):
                        if k == 2:
                            add_parts(r, off - 1)
                        if k == 3:
                            add_residual(r, off - 1)
                        if k == 4:
                            normalise(r, off - 1)
                if does(t, 2):
                    find_scale(r, off + 2)

            periods(dve, period)

        @block.tensor
        def _(pe):
            pe.wait_ge(ident16_ready, 1)

            def turn(r, off, k):
                m = len(BY_PE) * value(r, off) + PE_ORDER.index(k)
                since = next(n for n in range(1, len(BY_PE) + 1)
                             if BY_PE[PE_ORDER[(PE_ORDER.index(k) - n) % len(BY_PE)]] == BY_PE[k])
                pe.wait_ge(lo_ready, STEPS * value(r, off) + k + 1)
                if not (isinstance(r, int) and m < since):
                    pe.wait_ge(evacuated, m - since + 1)
                for i in range(2 * TILES):
                    a, at = i // TILES, i % TILES * P
                    mm = pe.transpose(turned[BY_PE[k]][:, i * P:(i + 1) * P],
                                      parts[:, k % RING, a, at:at + P], ident16[:, :])
                mm.then_inc(pe_turned, 1)

            def turned_by(r, off, k):
                if k in BY_PE:
                    pe.wait_ge(evacuated, len(BY_PE) * value(r, off) + PE_ORDER.index(k) + 1)
                else:
                    transposed_by(pe, r, off, k)

            def period(r, off, t):
                if does(t, 0):
                    pe.wait_ge(slots_free, value(r, off) + 1)
                for k in range(STEPS):
                    o, there, kk = ahead(off, t, k, PE_AHEAD)
                    if there and kk in BY_PE:
                        turn(r, o, kk)
                    if not does(t, 0):
                        continue
                    turned_by(r, off, k)
                    for i in range(TILES):
                        j = k * TILES + i
                        tile = slice(i * P, (i + 1) * P)
                        pe.matmul(acc[off % SLOTS][:, :], aT[:, k % RING, 0, tile],
                                  support[:, j, :, :].rearrange("p a d -> p (a d)"),
                                  start=(j == 0), stop=(j == NB - 1), skip_group_check=True)
                        mm = pe.matmul(acc[off % SLOTS][:, D:2 * D], aT[:, k % RING, 1, tile],
                                       support[:, j, 0, :], start=False, stop=(j == NB - 1),
                                       skip_group_check=True)
                    mm.then_inc(multiplied, 1)

            periods(pe, period)


def kernel(**inputs):
    import numpy as np
    import concourse.bacc as bacc
    from concourse.bass_utils import run_bass_kernel_spmd

    nc = bacc.Bacc("TRN2", target_bir_lowering=False, num_devices=1, dynamic_dma_scratch_size=1024)
    arrays, args = {}, []
    for name in ("x", "adj", "L0_gnn_H_v", "L1_gnn_W"):
        a = np.ascontiguousarray(inputs[name])
        arrays[f"in_{name}"] = a
        args.append(nc.dram_tensor(f"in_{name}", a.shape, mybir.dt.from_np(a.dtype),
                                   kind="ExternalInput").ap())
    out = nc.dram_tensor("out_0", (N, D), F32, kind="ExternalOutput").ap()
    graph_network(nc, *args, out)
    r = run_bass_kernel_spmd(nc, [arrays], core_ids=[0])
    return r.results[0]["out_0"]
```
